# Optimizing a Trainium2 kernel written in Bass

```python
import numpy as np
import jax
import jax.numpy as jnp

def _softmax(x, axis=-1):
    return jax.nn.softmax(x, axis=axis)

def _gelu(x):
    return jax.nn.gelu(x, approximate=True)

def _silu(x):
    return jax.nn.silu(x)

def _sigmoid(x):
    return jax.nn.sigmoid(x)

def _layernorm(x, axis=-1, eps=1e-05):
    m = jnp.mean(x, axis=axis, keepdims=True)
    v = jnp.var(x, axis=axis, keepdims=True)
    return (x - m) / jnp.sqrt(v + eps)

def _scatter_add(tgt, idx, src, axis=0):
    return tgt.at[idx].add(src)

def _segment_sum(src, seg, n):
    return jax.ops.segment_sum(src, seg, n)
kernel_name = 'mk_adaln_d1_jaxref_r8_c9245c'

def setup_inputs(seed: int=0):
    np.random.seed(seed)
    _w = jnp.asarray

    def _L0_attn_setup():
        import jax, jax.numpy as jnp
        import numpy as np
        HEAD_NUM = 16
        ROPE_BASE = 10000.0

        def _rotate_half(x):
            x_even = x[..., ::2]
            x_odd = x[..., 1::2]
            return jnp.stack((-x_odd, x_even), axis=-1).reshape(x.shape)

        def _rope_cos_sin(seq_len, head_dim):
            half = head_dim // 2
            inv_freq = 1.0 / ROPE_BASE ** (jnp.arange(half, dtype=jnp.float32) / half)
            t = jnp.arange(seq_len, dtype=jnp.float32)
            freqs = t[:, None] * inv_freq[None, :]
            cos = jnp.repeat(jnp.cos(freqs), 2, axis=-1)
            sin = jnp.repeat(jnp.sin(freqs), 2, axis=-1)
            return (cos, sin)
        key = jax.random.key(seed)
        ks = jax.random.split(key, 9)
        B, S, H = (2, 256, 256)
        std = 1.0 / np.sqrt(H)
        return {'x': jax.random.normal(ks[0], (B, S, H), jnp.float32), 'Wq': jax.random.normal(ks[1], (H, H), jnp.float32) * std, 'bq': jax.random.normal(ks[2], (H,), jnp.float32) * std, 'Wk': jax.random.normal(ks[3], (H, H), jnp.float32) * std, 'bk': jax.random.normal(ks[4], (H,), jnp.float32) * std, 'Wv': jax.random.normal(ks[5], (H, H), jnp.float32) * std, 'bv': jax.random.normal(ks[6], (H,), jnp.float32) * std, 'Wo': jax.random.normal(ks[7], (H, H), jnp.float32) * std, 'bo': jax.random.normal(ks[8], (H,), jnp.float32) * std}
    _L0_attn_in = _L0_attn_setup()

    def _L0_ffn_setup():
        import jax, jax.numpy as jnp
        import numpy as np
        TOP_K = 8
        CAPACITY = 128
        key = jax.random.key(seed)
        k1, k2, k3, k4 = jax.random.split(key, 4)
        B, S, H, E, I = (2, 128, 256, 64, 96)
        hidden_states = jax.random.normal(k1, (B, S, H), dtype=jnp.float32)
        router_weight = jax.random.normal(k2, (E, H), dtype=jnp.float32) * 0.02
        gate_up_proj = jax.random.normal(k3, (E, H, 2 * I), dtype=jnp.float32) * 0.02
        down_proj = jax.random.normal(k4, (E, I, H), dtype=jnp.float32) * 0.02
        return {'hidden_states': hidden_states, 'router_weight': router_weight, 'gate_up_proj': gate_up_proj, 'down_proj': down_proj}
    _L0_ffn_in = _L0_ffn_setup()
    _L0_c = _w((lambda *s: np.random.randn(*s).astype(np.float32) * 0.05)(4, 256))
    _L0_wmod = _w((lambda *s: np.random.randn(*s).astype(np.float32) * 0.05)(256, 6 * 256) * 256 ** (-0.5))
    _d = {'L0_attn_x': _L0_attn_in['x'], 'L0_attn_Wq': _L0_attn_in['Wq'], 'L0_attn_bq': _L0_attn_in['bq'], 'L0_attn_Wk': _L0_attn_in['Wk'], 'L0_attn_bk': _L0_attn_in['bk'], 'L0_attn_Wv': _L0_attn_in['Wv'], 'L0_attn_bv': _L0_attn_in['bv'], 'L0_attn_Wo': _L0_attn_in['Wo'], 'L0_attn_bo': _L0_attn_in['bo'], 'L0_ffn_router_weight': _L0_ffn_in['router_weight'], 'L0_ffn_gate_up_proj': _L0_ffn_in['gate_up_proj'], 'L0_ffn_down_proj': _L0_ffn_in['down_proj'], 'L0_c': _L0_c, 'L0_wmod': _L0_wmod}
    _x0 = _d['L0_attn_x']
    _d['L0_attn_x'] = jax.random.normal(jax.random.fold_in(jax.random.key(seed), 1), (4, 256, 256), dtype=_x0.dtype)
    del _x0
    return _d

def reference(L0_attn_x, L0_attn_Wq, L0_attn_bq, L0_attn_Wk, L0_attn_bk, L0_attn_Wv, L0_attn_bv, L0_attn_Wo, L0_attn_bo, L0_ffn_router_weight, L0_ffn_gate_up_proj, L0_ffn_down_proj, L0_c, L0_wmod):

    def _L0_attn_ref(x, Wq, bq, Wk, bk, Wv, bv, Wo, bo):
        import jax, jax.numpy as jnp
        import numpy as np
        HEAD_NUM = 16
        ROPE_BASE = 10000.0

        def _rotate_half(x):
            x_even = x[..., ::2]
            x_odd = x[..., 1::2]
            return jnp.stack((-x_odd, x_even), axis=-1).reshape(x.shape)

        def _rope_cos_sin(seq_len, head_dim):
            half = head_dim // 2
            inv_freq = 1.0 / ROPE_BASE ** (jnp.arange(half, dtype=jnp.float32) / half)
            t = jnp.arange(seq_len, dtype=jnp.float32)
            freqs = t[:, None] * inv_freq[None, :]
            cos = jnp.repeat(jnp.cos(freqs), 2, axis=-1)
            sin = jnp.repeat(jnp.sin(freqs), 2, axis=-1)
            return (cos, sin)
        B, S, H = x.shape
        nh = HEAD_NUM
        d = H // nh
        scale = jnp.float32(np.sqrt(d))

        def proj(W, b):
            y = x @ W.T + b
            return y.reshape(B, S, nh, d).transpose(0, 2, 1, 3)
        Q = proj(Wq, bq)
        K = proj(Wk, bk)
        V = proj(Wv, bv)
        cos, sin = _rope_cos_sin(S, d)
        Q = Q * cos + _rotate_half(Q) * sin
        K = K * cos + _rotate_half(K) * sin
        scores = jnp.einsum('bhqd,bhkd->bhqk', Q, K) / scale
        causal = jnp.tril(jnp.ones((S, S), dtype=bool))
        scores = jnp.where(causal, scores, jnp.float32(-jnp.inf))
        attn = jax.nn.softmax(scores, axis=-1)
        out = jnp.einsum('bhqk,bhkd->bhqd', attn, V)
        out = out.transpose(0, 2, 1, 3).reshape(B, S, H)
        return out @ Wo.T + bo

    def _L0_ffn_ref(hidden_states, router_weight, gate_up_proj, down_proj):
        import jax, jax.numpy as jnp
        import numpy as np
        TOP_K = 8
        CAPACITY = 128
        B, S, H = hidden_states.shape
        E = router_weight.shape[0]
        K, C = (TOP_K, CAPACITY)
        x = hidden_states.reshape(-1, H)
        logits = x @ router_weight.T
        probs = jax.nn.softmax(logits, axis=-1)
        topw, topi = jax.lax.top_k(probs, K)
        topw = topw / jnp.sum(topw, axis=-1, keepdims=True)
        flat_e = topi.reshape(-1)
        oh = jax.nn.one_hot(flat_e, E, dtype=jnp.int32)
        pos = jnp.take_along_axis(jnp.cumsum(oh, axis=0), flat_e[:, None], axis=1)[:, 0] - 1
        x_rep = jnp.repeat(x, K, axis=0)
        xe = jnp.zeros((E, C, H), x.dtype).at[flat_e, pos].set(x_rep, mode='drop')
        gu = jnp.einsum('ech,ehf->ecf', xe, gate_up_proj)
        g, u = jnp.split(gu, 2, axis=-1)
        h = jax.nn.silu(g) * u
        ye = jnp.einsum('eci,eih->ech', h, down_proj)
        valid = pos < C
        y_flat = jnp.where(valid[:, None], ye[flat_e, jnp.minimum(pos, C - 1)], 0.0)
        y = jnp.sum(y_flat.reshape(-1, K, H) * topw.reshape(-1, K)[..., None], axis=1)
        return y.reshape(B, S, H)
    x = L0_attn_x
    mod = (_silu(L0_c) @ L0_wmod).reshape(L0_c.shape[0], 6, 1, -1)
    sa, ca, ga, sb, cb, gb = (mod[:, 0], mod[:, 1], mod[:, 2], mod[:, 3], mod[:, 4], mod[:, 5])
    ga = (2 * (ga >= 0) - 1) * jnp.maximum(jnp.abs(ga), 0.25)
    gb = (2 * (gb >= 0) - 1) * jnp.maximum(jnp.abs(gb), 0.25)
    h = _layernorm(x, axis=-1) * (1 + ca) + sa
    x = x + ga * _L0_attn_ref(h, L0_attn_Wq, L0_attn_bq, L0_attn_Wk, L0_attn_bk, L0_attn_Wv, L0_attn_bv, L0_attn_Wo, L0_attn_bo)
    h = _layernorm(x, axis=-1) * (1 + cb) + sb
    x = x + gb * _L0_ffn_ref(h, L0_ffn_router_weight, L0_ffn_gate_up_proj, L0_ffn_down_proj)
    return x

_drawn_inputs = setup_inputs


def setup_inputs(seed=0):
    import zlib

    import numpy as np

    out = dict(_drawn_inputs(seed))
    spreads = {}
    factors = {'L0_attn_bq': 8.0,
     'L0_attn_bk': 8.0,
     'L0_attn_bv': 3.63,
     'L0_attn_bo': 3.779,
     'L0_ffn_router_weight': 8.0,
     'L0_ffn_gate_up_proj': 8.0,
     'L0_ffn_down_proj': 8.0}
    for name, (base, spread) in spreads.items():
        noise = np.random.default_rng([zlib.crc32(name.encode()), seed]).standard_normal(out[name].shape)
        drawn = base * np.exp(spread * noise) if base else spread * noise
        out[name] = jnp.asarray(drawn.astype(out[name].dtype))
    for name, factor in factors.items():
        out[name] = (out[name] * factor).astype(out[name].dtype)
    return out
```

```python
import concourse.bass as bass
from concourse import mybir
from contextlib import ExitStack


def adaln_moe_program(nc, x, wqkvT, bias, woT, routerT, gate_up, down, cond, wmod,
                      rope, consts, token_ids, out):
    FP32, BF16, FP16 = mybir.dt.float32, mybir.dt.bfloat16, mybir.dt.float16
    I32, U32 = mybir.dt.int32, mybir.dt.uint32
    ACT, ALU, AX = mybir.ActivationFunctionType, mybir.AluOpType, mybir.AxisListType

    B, S, H = x.shape
    P = 128
    TPB = S // P
    HC = H // P
    NH = 16
    D = H // NH
    E, _, GU = gate_up.shape
    I = GU // 2
    K = 8
    CAP = 128
    TOK = B * S
    SLOTS = E * CAP
    ROW = H + 4
    NACC = 4
    ACCROWS = TOK + CAP
    EW = HC * (GU + 1) + H
    EARLY = 32
    GRP = 8
    SCALE = 1.0 / float(D) ** 0.5
    EPS = 1e-5
    FAR = -3.0e38
    BIGSLOT = 2 * SLOTS

    slot_rows = nc.dram_tensor("slot_rows", [SLOTS, ROW], FP32, kind="Internal").ap()
    sums = [nc.dram_tensor(f"sum{a}", [ACCROWS, H], FP32, kind="Internal").ap() for a in range(NACC)]
    mod_dram = nc.dram_tensor("mod_rows", [B, 6 * H], FP32, kind="Internal").ap()

    ctx = ExitStack()
    with ctx:
        def sb(name, shape, dt=FP32):
            return ctx.enter_context(nc.sbuf_tensor(name, shape, dt))

        def sem(name):
            return ctx.enter_context(nc.semaphore(name))

        arena = sb("arena", [P, E * EW])
        x_sb = sb("x_sb", [P, B * TPB, H])
        gbB = sb("gbB", [P, B, H])
        rows = sb("rows", [P, TPB, ROW])
        cst = sb("cst", [P, 4 * P + NH + E])
        ident = cst[:, 0:P]
        tok = sb("tok", [P, B * TPB + 1], I32)
        router_sb = sb("router_sb", [P, HC, E])
        zero_row = sb("zero_row", [P, ROW])

        expert_w = arena[:, :].rearrange("p (e w) -> p e w", w=EW)

        NXE = 8
        stage = sb("stage", [P, NXE * (ROW + 1) + 2 * HC * CAP + 6 * I + 2 * CAP + NACC * H])

        def region(whole, at, limit):
            cur = [at]

            def take(shape, dt=FP32, parts=P):
                n = 1
                for d in shape:
                    n *= d
                w = n * (2 if dt in (BF16, FP16) else 4) // 4
                v = whole[0:parts, cur[0]:cur[0] + w]
                cur[0] += w
                assert cur[0] <= limit
                v = v if dt == FP32 else v.bitcast(dt)
                names = "abcde"[:len(shape)]
                if len(shape) == 1:
                    return v
                return v.rearrange("p (" + " ".join(names) + ") -> p " + " ".join(names), **dict(zip(names, shape)))
            return take

        ffn = region(stage, 0, stage.shape[1])
        xe = ffn([NXE, ROW])
        xeT = ffn([2, HC * CAP])
        expg = ffn([2, I])
        hid0 = ffn([2, I])
        hid = ffn([2, I])
        hidT = ffn([2, CAP], parts=I)
        gatew = ffn([NXE])
        ye = ffn([NACC, H])

        SC = TPB * S - P
        scratch = region(arena, EARLY * EW, E * EW)
        probT = scratch([2, 4 * SC])
        v_aug = scratch([TPB, NH, 32])
        qT = scratch([NH // 2, S], FP16)
        kT = scratch([NH // 2, S], FP16)
        h1T = scratch([HC, S])
        xn = scratch([TPB, H])
        rope1 = scratch([2 * H])
        rope2 = scratch([2 * H])
        q_split = scratch([TPB, NH, 4, D], FP16)
        k_split = scratch([TPB, NH, 4, D], FP16)
        att_sb = scratch([2, 512])
        att_tok = scratch([TPB, H])
        attT = scratch([HC, S])
        wqkv_sb = scratch([HC, 3 * H])
        wo_sb = scratch([HC, H])
        modB = scratch([B, 3 * H])
        h2T = h1T
        before = region(arena, EARLY * EW, EARLY * EW + 2 * 4 * SC)
        wmod_sb = before([HC, 6 * H])
        at = EARLY * EW + 2 * 4 * SC + TPB * NH * 32
        before = region(arena, at, at + NH * S)
        bias_p = before([3, 4 * H], BF16, parts=1)
        at += NH * S // 2
        before = region(arena, at, at + 2 * TPB * H)
        cond_sb = before([4, H], parts=B)
        at += HC * S
        before = region(arena, at, at + TPB * H)
        mod_t = before([2, H], parts=B)
        at += TPB * H
        before = region(arena, at, at + 6 * H)
        mod_sb = before([6 * H], parts=B)
        at += 4 * H + TPB * NH * 4 * D
        before = region(arena, at, at + 8 * H)
        bias_f = before([2, 4 * H], parts=1)

        early = region(stage, 0, stage.shape[1])
        rope_sb = sb("rope_sb", [P, TPB, 2, D])
        ident16 = early([P], FP16)
        identb = early([P], BF16)
        maskb = early([P], BF16)
        maskTb = early([P], BF16)
        prefixb = early([P], BF16)
        onesb = early([P], BF16)
        pickb = early([NH, P], BF16)
        ones3 = early([P], BF16, parts=3)
        bias3 = early([4 * H], BF16, parts=3)
        condT = sb("condT", [P, HC, B])
        modT = sb("modT", [P, 4, B])
        stats = sb("stats", [P, B * TPB, 6])
        mv1 = sb("mv1", [P, B * TPB, 2])
        rs1 = sb("rs1", [P, 4, B * TPB])
        mv2 = sb("mv2", [P, TPB, 2])
        rs2 = sb("rs2", [P, 4, TPB])
        rmax = sb("rmax", [P, TPB, NH])
        negr = early([2, TPB, NH])
        neg3 = early([TPB, 2, 4, NH], BF16)
        negT = early([S], BF16)
        rden = sb("rden", [P, TPB, NH])
        logit = early([TPB, E])
        logit_rep = early([TPB, E])
        top8 = sb("top8", [P, TPB, K])
        exp8 = sb("exp8", [P, TPB, K])
        sum8 = sb("sum8", [P, TPB])
        sel = early([TPB, E], BF16)
        seen = early([TPB + 1, E], BF16)
        code = early([2, TPB, E])
        code8 = sb("code8", [P, TPB, K])
        slot_idx = sb("slot_idx", [P, TPB, K], U32)

        bank = [ctx.enter_context(nc.psum_tensor(f"bank{i}", [P, 512], FP32)) for i in range(8)]
        bank16 = [b[:, :].bitcast(FP16) for b in bank]
        bankb = [b[:, :].bitcast(BF16) for b in bank]

        s_c = sem("consts_loaded")
        s_m = sem("wmod_loaded")
        s_x = sem("x_loaded")
        s_w = sem("attn_weights_loaded")
        s_bias = sem("bias_loaded")
        s_b3 = sem("bias3_moved")
        s_md = sem("mod_stored")
        s_mb = sem("mod_broadcast")
        s_ew = sem("early_experts_loaded")
        s_lw = sem("late_experts_loaded")
        s_fill = sem("slots_filled")
        s_zero = sem("zero_row_ready")
        vch = sem("vector_chain")
        ach = sem("scalar_chain")
        gch = sem("gpsimd_chain")
        v_csts = sem("consts_converted")
        a_econd = sem("exp_cond")
        v_silu = sem("silu_ready")
        p_condT = sem("condT_in_bank")
        v_condT = sem("condT_ready")
        p_mod = sem("mod_in_banks")
        v_mod = sem("mod_ready")
        p_modT = sem("modT_in_bank")
        v_modT = sem("modT_ready")
        g_bias = sem("bias_split")
        v_var1 = sem("variance1_ready")
        a_rs1 = sem("rstd1_guess")
        v_xn = sem("xn_ready")
        p_xnT = sem("xnT_in_bank")
        a_h1T = sem("h1T_ready")
        p_qkv = sem("qkv_in_banks")
        v_rope = sem("rope_ready")
        a_hi = sem("high_parts_ready")
        v_split = sem("split_ready")
        v_vaug = sem("v_ready")
        p_qkT = sem("qkT_in_banks")
        v_qT = sem("qT_ready")
        a_kT = sem("kT_ready")
        p_s1 = sem("scores_for_max")
        v_max = sem("max_taken")
        v_neg = sem("neg_max_split")
        p_negT = sem("neg_max_T")
        a_negT = sem("neg_max_T_ready")
        p_s2 = sem("scoresT_in_bank")
        a_exp = sem("probs_ready")
        p_pv = sem("pv_done")
        a_att = sem("att_copied")
        p_attq = sem("att_token_major")
        v_att = sem("att_normalised")
        p_attT = sem("attT_in_bank")
        a_attT = sem("attT_ready")
        p_o = sem("o_proj_done")
        v_x2 = sem("x2_variance")
        a_rs2 = sem("rstd2_guess")
        v_h2 = sem("h2_ready")
        p_h2T = sem("h2T_in_bank")
        a_h2T = sem("h2T_ready")
        p_log = sem("logits_in_bank")
        v_top = sem("top8_ready")
        a_sum = sem("sum8_ready")
        v_sel = sem("picks_ready")
        p_cum = sem("ranks_in_bank")
        v_slot = sem("slots_ready")
        g_scat = sem("rows_scattered")
        g_rcol = sem("router_columns")
        xe_ld = [sem(f"slot_rows_loaded{j}") for j in range(NXE)]
        p_xeT = sem("xeT_in_bank")
        a_xeT = sem("xeT_ready")
        p_gu = sem("gate_up_in_bank")
        a_eg = sem("exp_gate_ready")
        a_w = sem("gate_weight_ready")
        v_hid = sem("hidden_ready")
        p_hidT = sem("hiddenT_in_bank")
        a_hidT = sem("hiddenT_ready")
        p_ye = sem("expert_out_in_bank")
        v_ye = sem("expert_out_ready")
        added = [sem(f"added{a}") for a in range(NACC)]
        sum_ld = sem("sums_loaded")
        v_out = sem("out_ready")
        s_out = sem("out_stored")

        groups = [[par + 8 * half + 2 * i for i in range(4)] for par in range(2) for half in range(2)]
        row0 = [64 * (g // 2) for g in range(4)]

        block = ctx.enter_context(nc.Block())

        def linker(eng, chain):
            n = [0]

            def link(ins):
                n[0] += 1
                ins.then_inc(chain, 1)
                eng.wait_ge(chain, n[0])

            def clear():
                eng.sem_clear(chain)
                n[0] = 0
            return link, clear

        @block.sync
        def _(sp):
            sp.dma_start(cst[:, :], consts).then_inc(s_c, 16)
            sp.dma_start(tok[:, :], token_ids).then_inc(s_c, 16)
            sp.dma_start(cond_sb[:, 0, :], cond).then_inc(s_c, 16)
            sp.dma_start(rope_sb[:, :, :, :], rope.rearrange("(t p) a d -> p t a d", p=P)).then_inc(s_c, 16)
            sp.dma_start(wmod_sb, wmod.rearrange("(k p) n -> p k n", p=P)).then_inc(s_m, 16)
            sp.dma_start(x_sb[:, :, :], x.rearrange("b (t p) h -> p (b t) h", p=P)).then_inc(s_x, 16)
            sp.dma_start(bias_f[0:1, 0, :], bias).then_inc(s_bias, 16)
            sp.dma_start(wqkv_sb, wqkvT.rearrange("(k p) n -> p k n", p=P)).then_inc(s_w, 16)
            sp.dma_start(wo_sb, woT.rearrange("(k p) n -> p k n", p=P)).then_inc(s_w, 16)
            sp.dma_start(router_sb[:, :, :], routerT.rearrange("(k p) n -> p k n", p=P)).then_inc(s_w, 16)
            sp.wait_ge(g_bias, 1)
            sp.dma_start(bias3, bias_p[0:1, :, :]).then_inc(s_b3, 16)

            def load_experts(e0, s):
                e1 = e0 + GRP
                for k in range(HC):
                    sp.dma_start(expert_w[:, e0:e1, k * (GU + 1):k * (GU + 1) + GU],
                                 gate_up[e0:e1, k * P:(k + 1) * P, :].rearrange("e p f -> p e f")).then_inc(s, 16)
                sp.dma_start(expert_w[0:I, e0:e1, HC * (GU + 1):EW],
                             down[e0:e1, :, :].rearrange("e i h -> i e h")).then_inc(s, 16)

            sp.wait_ge(v_mod, 1)
            sp.dma_start(mod_dram, mod_sb).then_inc(s_md, 16)
            sp.wait_ge(s_md, 16)
            sp.dma_start(modB, mod_dram[None, :, 2 * H:5 * H].broadcast_to([P, B, 3 * H])).then_inc(s_mb, 16)
            sp.dma_start(gbB[:, :, :], mod_dram[None, :, 5 * H:6 * H].broadcast_to([P, B, H])).then_inc(s_mb, 16)
            sp.wait_ge(s_zero, 1)
            for n in range(8):
                sp.dma_start(slot_rows[n * 1024:(n + 1) * 1024, :].rearrange("(e c) r -> c e r", c=CAP),
                             zero_row[:, None, :].broadcast_to([P, 8, ROW])).then_inc(s_fill, 16)
            for a in range(NACC):
                sp.dma_start(sums[a].rearrange("(n p) h -> p n h", p=P),
                             zero_row[:, None, 0:H].broadcast_to([P, ACCROWS // P, H])).then_inc(s_fill, 16)
            for e0 in range(0, EARLY, GRP):
                load_experts(e0, s_ew)
            sp.wait_ge(g_scat, 16 * K * B * TPB)

            def load_slots(i, j, first):
                e = GRP * i + j
                if not first:
                    sp.wait_ge(added[j % NACC], 16 * (2 * i - 1 + j // NACC))
                sp.dma_start(xe[:, j, :], slot_rows.rearrange("(e c) r -> c e r", c=CAP)[:, e, :]).then_inc(xe_ld[j], 16)

            for j in range(GRP):
                load_slots(0, j, True)
            for e0 in range(EARLY, E, GRP):
                load_experts(e0, s_lw)
            with sp.Fori(1, E // GRP) as i:
                for j in range(GRP):
                    load_slots(i, j, False)
            for a in range(NACC):
                sp.wait_ge(added[a], 16 * (E // NACC))
                sp.dma_start(arena[:, a * TOK * 2:(a + 1) * TOK * 2].rearrange("p (t h) -> p t h", h=H),
                             sums[a][0:TOK, :].rearrange("(t p) h -> p t h", p=P)).then_inc(sum_ld, 16)
            for b in range(B):
                sp.wait_ge(v_out, b + 1)
                sp.dma_start(out[b].rearrange("(t p) h -> p t h", p=P), x_sb[:, bass.ts(b, TPB), :]).then_inc(s_out, 16)
            sp.wait_ge(s_out, 16 * B)

        @block.gpsimd
        def _(pool):
            link, clear = linker(pool, gch)
            link(nc.gpsimd.memset(zero_row[:, :], 0.0))
            pool.wait_ge(s_c, 64)
            nc.gpsimd.tensor_copy(zero_row[:, H + 2:H + 3].bitcast(I32), tok[:, B * TPB:B * TPB + 1]).then_inc(s_zero, 1)
            link(nc.gpsimd.memset(rows[:, :, H + 3:H + 4], 0.0))
            pool.wait_ge(s_bias, 16)
            link(nc.gpsimd.tensor_copy(bias_p[0:1, 0, :], bias_f[0:1, 0, :]))
            link(nc.gpsimd.tensor_tensor(bias_f[0:1, 1, :], bias_f[0:1, 0, :], bias_p[0:1, 0, :], ALU.subtract))
            link(nc.gpsimd.tensor_copy(bias_p[0:1, 1, :], bias_f[0:1, 1, :]))
            link(nc.gpsimd.tensor_tensor(bias_f[0:1, 0, :], bias_f[0:1, 1, :], bias_p[0:1, 1, :], ALU.subtract))
            nc.gpsimd.tensor_copy(bias_p[0:1, 2, :], bias_f[0:1, 0, :]).then_inc(g_bias, 1)
            pool.wait_ge(s_w, 48)

            def router_columns(e0, e1):
                for k in range(HC):
                    c = k * (GU + 1) + GU
                    nc.gpsimd.tensor_copy(expert_w[:, e0:e1, c:c + 1],
                                          router_sb[:, k, e0:e1].rearrange("p (e o) -> p e o", o=1)).then_inc(g_rcol, 1)

            router_columns(0, EARLY)
            pool.wait_ge(s_fill, 16 * (8 + NACC))

            def scatter(b):
                for t in range(TPB):
                    pool.wait_ge(v_slot, TPB * b + t + 1)
                    for k in range(K):
                        pool.indirect_dma_start(
                            slot_rows, bass.IndirectOffsetOnAxis(ap=slot_idx[:, t, k:k + 1], axis=0),
                            rows[:, t, :], None, bounds_check=SLOTS - 1, oob_is_err=False).then_inc(g_scat, 16)

            for b in range(B):
                scatter(b)
            pool.wait_ge(g_scat, 16 * K * B * TPB)
            router_columns(EARLY, E)

            def add_expert(i, j, first):
                e = GRP * i + j
                pool.wait_ge(v_ye, e + 1)
                if not (first and j < NACC):
                    pool.wait_ge(added[j % NACC], 16 * (2 * i + j // NACC))
                pool.indirect_dma_start(
                    sums[j % NACC], bass.IndirectOffsetOnAxis(ap=xe[:, j, H + 2:H + 3].bitcast(U32), axis=0),
                    ye[:, j % NACC, :], None, bounds_check=ACCROWS - 1, oob_is_err=True,
                    compute_op=ALU.add).then_inc(added[j % NACC], 16)

            for e in range(E):
                add_expert(e // GRP, e % GRP, e < GRP)

        @block.scalar
        def _(act):
            link, clear = linker(act, ach)
            act.wait_ge(s_c, 64)
            nc.scalar.activation(cond_sb[:, 1, :], cond_sb[:, 0, :], ACT.Exp, scale=-1.0).then_inc(a_econd, 1)
            act.wait_ge(v_var1, 1)
            link(nc.scalar.activation(rs1[:, 1, :], rs1[:, 0, :], ACT.Ln))
            nc.scalar.activation(rs1[:, 2, :], rs1[:, 1, :], ACT.Exp, scale=-0.5).then_inc(a_rs1, 1)
            act.wait_ge(v_modT, 1)
            act.wait_ge(v_csts, 1)

            def front(it):
                act.wait_ge(p_xnT, it + 1)
                for k in range(HC):
                    nc.scalar.activation(h1T[:, k, :], bank[0][:, k * S:(k + 1) * S], ACT.Identity,
                                         bias=modT[:, k, bass.ts(it, 1)], scale=modT[:, 2 + k, bass.ts(it, 1)]).then_inc(a_h1T, 1)

            def high(it, t):
                act.wait_ge(v_rope, TPB * it + t + 1)
                nc.scalar.activation(q_split[:, t, :, 0, :], rope1[:, 0:H].rearrange("p (h d) -> p h d", d=D),
                                     ACT.Copy).then_inc(a_hi, 1)
                nc.scalar.activation(k_split[:, t, :, 0, :], rope1[:, H:2 * H].rearrange("p (h d) -> p h d", d=D),
                                     ACT.Copy).then_inc(a_hi, 1)

            def softmax(b, it):
                n = 0
                for g in range(4):
                    if g >= 2:
                        act.wait_ge(p_pv, 4 * b + g - 1)
                    for part in range(3):
                        act.wait_ge(p_s2, 12 * b + n + 1)
                        dst = probT[:, g % 2, part * 512:(part + 1) * 512]
                        nc.scalar.activation(dst, bank[4 + n % 3][:, :], ACT.Exp, scale=SCALE).then_inc(a_exp, 1)
                        n += 1
                    if it is not None and g < 2:
                        high(it, g)
                    if g % 2:
                        act.wait_ge(p_pv, 4 * b + g + 1)
                        nc.scalar.activation(att_sb[:, g // 2, :], bank[7][:, :], ACT.Copy).then_inc(a_att, 1)

            def k_copies(it):
                for t in range(TPB):
                    act.wait_ge(p_qkT, 4 * it + 2 * t + 2)
                    src = bank16[(2, 0)[t]].rearrange("p (g q) -> p g q", q=P)
                    nc.scalar.activation(kT[:, :, t * P:(t + 1) * P], src, ACT.Copy).then_inc(a_kT, 1)

            def back(b):
                for t in range(TPB):
                    act.wait_ge(p_attT, TPB * b + t + 1)
                    src = bank[0][:, :].rearrange("p (k q) -> p k q", k=HC)
                    nc.scalar.activation(attT[:, :, t * P:(t + 1) * P], src[:, :, t * P:(t + 1) * P],
                                         ACT.Copy).then_inc(a_attT, 1)
                act.wait_ge(v_x2, b + 1)
                link(nc.scalar.activation(rs2[:, 1, :], rs2[:, 0, :], ACT.Ln))
                nc.scalar.activation(rs2[:, 2, :], rs2[:, 1, :], ACT.Exp, scale=-0.5).then_inc(a_rs2, 1)
                act.wait_ge(p_h2T, b + 1)
                nc.scalar.activation(h2T[:, :, :], bank[0][:, :].rearrange("p (k q) -> p k q", k=HC),
                                     ACT.Copy).then_inc(a_h2T, 1)
                act.wait_ge(v_top, b + 1)
                for t in range(TPB):
                    nc.scalar.activation(exp8[:, t, :], top8[:, t, :], ACT.Exp, bias=rows[:, t, H:H + 1],
                                         accum_out=sum8[:, t:t + 1]).then_inc(a_sum, 1)

            def negs(it):
                act.wait_ge(p_negT, it + 1)
                nc.scalar.activation(negT, bankb[0][:, 0:S], ACT.Copy).then_inc(a_negT, 1)

            front(0)
            high(0, 0)
            high(0, 1)
            k_copies(0)
            negs(0)
            with act.Fori(1, B) as it:
                clear()
                front(it)
                softmax(it - 1, it)
                k_copies(it)
                back(it - 1)
                negs(it)
            clear()
            softmax(B - 1, None)
            back(B - 1)

            def expert_steps(i, j, first, last):
                s = GRP * i + j
                if not last:
                    act.wait_ge(p_xeT, s + 1)
                    if not (first and j < 2):
                        act.wait_ge(p_gu, s - 1)
                    nc.scalar.activation(xeT[:, j % 2, :], bank[j % 2][:, 0:HC * CAP], ACT.Copy).then_inc(a_xeT, 1)
                if not (first and j < 1) and not (last and j > 0):
                    q = (j - 1) % GRP
                    act.wait_ge(p_gu, s)
                    if not (first and j < 3):
                        act.wait_ge(v_hid, s - 2)
                    nc.scalar.activation(expg[:, q % 2, :], bank[2 + q % 2][:, 0:I], ACT.Exp, scale=-1.0).then_inc(a_eg, 1)
                    if not (first and j < GRP + 1):
                        act.wait_ge(v_ye, s - GRP)
                    nc.scalar.activation(gatew[:, q:q + 1], bank[2 + q % 2][:, GU:GU + 1], ACT.Exp,
                                         bias=xe[:, q, H:H + 1]).then_inc(a_w, 1)
                if not (first and j < 2) and not (last and j > 1):
                    q = (j - 2) % GRP
                    act.wait_ge(p_hidT, s - 1)
                    if not (first and j < 4):
                        act.wait_ge(p_ye, s - 3)
                    nc.scalar.activation(hidT[:, q % 2, :], bank[4 + q % 2][0:I, 0:CAP], ACT.Copy).then_inc(a_hidT, 1)

            for j in range(GRP):
                expert_steps(0, j, True, False)
            with act.Fori(1, E // GRP) as i:
                for j in range(GRP):
                    expert_steps(i, j, False, False)
            for j in range(3):
                expert_steps(E // GRP, j, False, True)

        @block.tensor
        def _(pe):
            mm = nc.tensor.matmul
            pe.wait_ge(s_c, 64)
            pe.wait_ge(v_silu, 1)
            for k in range(HC):
                last = nc.tensor.transpose(bank[0][:, k * B:(k + 1) * B], cond_sb[:, 3, k * P:(k + 1) * P], ident[0:B, 0:B])
            last.then_inc(p_condT, 1)
            pe.wait_ge(v_condT, 1)
            pe.wait_ge(s_m, 16)
            for n in range(3):
                for k in range(HC):
                    last = mm(bank[1 + n][0:B, :], condT[:, k, :], wmod_sb[:, k, n * 512:(n + 1) * 512],
                              start=k == 0, stop=k == HC - 1)
            last.then_inc(p_mod, 1)
            pe.wait_ge(v_mod, 1)
            for n in range(4):
                last = nc.tensor.transpose(bank[4][:, n * B:(n + 1) * B], mod_sb[:, n * P:(n + 1) * P], ident[0:B, 0:B])
            last.then_inc(p_modT, 1)
            pe.wait_ge(v_csts, 1)

            def front(it):
                pe.wait_ge(v_xn, it + 1)
                for t in range(TPB):
                    for k in range(HC):
                        last = nc.tensor.transpose(bank[0][:, k * S + t * P:k * S + (t + 1) * P],
                                                   xn[:, t, k * P:(k + 1) * P], ident)
                last.then_inc(p_xnT, 1)
                pe.wait_ge(a_h1T, HC * (it + 1))
                pe.wait_ge(s_w, 48)
                pe.wait_ge(s_b3, 16)
                for t in range(TPB):
                    for dst, c0, c1 in ((bank[1 + t][:, :], 0, 2 * H), (bank[3][:, t * H:(t + 1) * H], 2 * H, 3 * H)):
                        for k in range(HC):
                            mm(dst, h1T[:, k, t * P:(t + 1) * P], wqkv_sb[:, k, c0:c1], start=k == 0, stop=False)
                        last = mm(dst, ones3, bias3[:, c0:c1], start=False, stop=True)
                    last.then_inc(p_qkv, 1)

            def split_transposes(it):
                for t in range(TPB):
                    pe.wait_ge(v_split, TPB * it + t + 1)
                    if t == 0:
                        pe.wait_ge(v_vaug, it + 1)
                    for src, bk in ((q_split, (1, 3)[t]), (k_split, (2, 0)[t])):
                        flat = src[:, t, :, :, :].rearrange("p h a c -> p (h a c)")
                        for g in range(NH // 2):
                            last = nc.tensor.transpose(bank16[bk][:, g * P:(g + 1) * P], flat[:, g * P:(g + 1) * P], ident16)
                        last.then_inc(p_qkT, 1)

            def scores_for_max(it, b):
                pe.wait_ge(v_qT, TPB * (it + 1))
                pe.wait_ge(a_kT, TPB * (it + 1))
                n = 0
                for g in range(4):
                    r = slice(row0[g], row0[g] + 64)
                    for heads, qt in ((groups[g], 0), (groups[g][0:2], 1), (groups[g][2:4], 1)):
                        bk = bank[4 + n % 3]
                        if n >= 3:
                            pe.wait_ge(v_max, 12 * it + n - 2)
                        elif b is not None:
                            pe.wait_ge(a_exp, 12 * b + 10 + n)
                        w = (qt + 1) * P
                        view = bk[:, 0:len(heads) * w].rearrange("p (h k) -> p h k", k=w)
                        mm(view[:, :, w - P:w], identb, maskb[:, None, :].broadcast_to([P, len(heads), P]),
                           start=True, stop=False, skip_group_check=True)
                        for i, h in enumerate(heads):
                            last = mm(view[:, i, :], qT[r, h // 2, qt * P:(qt + 1) * P], kT[r, h // 2, 0:w],
                                      start=False, stop=i == len(heads) - 1, skip_group_check=True)
                        last.then_inc(p_s1, 1)
                        n += 1

            def neg_transposes(it):
                pe.wait_ge(v_neg, it + 1)
                for t in range(TPB):
                    last = nc.tensor.transpose(bankb[0][:, t * P:(t + 1) * P],
                                               neg3[:, t, :, :, :].rearrange("p a c h -> p (a c h)"), identb)
                last.then_inc(p_negT, 1)

            def attend(b):
                pe.wait_ge(a_negT, b + 1)
                n = 0

                def pv(g):
                    pe.wait_ge(a_exp, 12 * b + 3 * g + 3)
                    if g == 2:
                        pe.wait_ge(a_att, 2 * b + 1)
                    for kt in range(TPB):
                        for i, h in enumerate(groups[g]):
                            c = (g % 2) * S
                            src = (probT[:, g % 2, i * S:(i + 1) * S] if kt == 0 else
                                   probT[:, g % 2, 4 * S + i * P:4 * S + (i + 1) * P])
                            last = mm(bank[7][32 * i:32 * i + 32, c + kt * P:c + S], v_aug[:, kt, h, :], src,
                                      start=kt == 0, stop=kt == TPB - 1, skip_group_check=True)
                    last.then_inc(p_pv, 1)

                for g in range(4):
                    r = slice(row0[g], row0[g] + 64)
                    rn = slice(row0[g], row0[g] + 48)
                    for heads, kt in ((groups[g][0:2], 0), (groups[g][2:4], 0), (groups[g], 1)):
                        bk = bank[4 + n % 3]
                        if n >= 3:
                            pe.wait_ge(a_exp, 12 * b + n - 2)
                        w = (TPB - kt) * P
                        view = bk[:, 0:len(heads) * w].rearrange("p (h q) -> p h q", q=w)
                        mm(view[:, :, 0:P], identb, maskTb[:, None, :].broadcast_to([P, len(heads), P]),
                           start=True, stop=False, skip_group_check=True)
                        for i, h in enumerate(heads):
                            mm(view[:, i, :], kT[r, h // 2, kt * P:(kt + 1) * P], qT[r, h // 2, kt * P:S],
                               start=False, stop=False, skip_group_check=True)
                            last = mm(view[:, i, :], pickb[rn, h, :], negT[rn, kt * P:S],
                                      start=False, stop=i == len(heads) - 1, skip_group_check=True)
                        last.then_inc(p_s2, 1)
                        n += 1
                    if g > 0:
                        pv(g - 1)
                pv(3)

            def back(b, it):
                pe.wait_ge(a_att, 2 * b + 2)
                for t in range(TPB):
                    for g in range(4):
                        last = nc.tensor.transpose(bank[1 + t][:, g * P:(g + 1) * P],
                                                   att_sb[:, g // 2, (g % 2) * S + t * P:(g % 2) * S + (t + 1) * P], ident)
                    last.then_inc(p_attq, 1)
                for t in range(TPB):
                    pe.wait_ge(v_att, TPB * b + t + 1)
                    for k in range(HC):
                        last = nc.tensor.transpose(bank[0][:, k * S + t * P:k * S + (t + 1) * P],
                                                   att_tok[:, t, k * P:(k + 1) * P], ident)
                    last.then_inc(p_attT, 1)
                    pe.wait_ge(a_attT, TPB * b + t + 1)
                    dst = bank[3][:, t * H:(t + 1) * H]
                    for k in range(HC):
                        mm(dst, attT[:, k, t * P:(t + 1) * P], wo_sb[:, k, :], start=k == 0, stop=False)
                    last = mm(dst, ones3, bias3[:, 3 * H:4 * H], start=False, stop=True)
                last.then_inc(p_o, 1)
                pe.wait_ge(v_h2, b + 1)
                for t in range(TPB):
                    for k in range(HC):
                        last = nc.tensor.transpose(bank[0][:, k * S + t * P:k * S + (t + 1) * P],
                                                   rows[:, t, k * P:(k + 1) * P], ident)
                last.then_inc(p_h2T, 1)
                pe.wait_ge(a_h2T, b + 1)
                for t in range(TPB):
                    for k in range(HC):
                        last = mm(bank[1][:, t * E:(t + 1) * E], h2T[:, k, t * P:(t + 1) * P], router_sb[:, k, :],
                                  start=k == 0, stop=k == HC - 1)
                last.then_inc(p_log, 1)
                pe.wait_ge(v_sel, b + 1)
                for t in range(TPB):
                    mm(bank[2][:, t * E:(t + 1) * E], prefixb, sel[:, t, :], start=True, stop=False)
                    last = mm(bank[2][:, t * E:(t + 1) * E], onesb, seen[:, t, :], start=False, stop=True)
                last.then_inc(p_cum, 1)

            front(0)
            split_transposes(0)
            scores_for_max(0, None)
            neg_transposes(0)
            with pe.Fori(1, B) as it:
                pe.wait_ge(a_negT, it)
                front(it)
                attend(it - 1)
                split_transposes(it)
                scores_for_max(it, it - 1)
                back(it - 1, it)
                neg_transposes(it)
            attend(B - 1)
            back(B - 1, None)

            pe.wait_ge(v_slot, TPB * B)
            pe.wait_ge(g_rcol, HC)
            pe.wait_ge(s_ew, 16 * 3 * EARLY // GRP)

            def expert_steps(i, j, first, last_):
                s = GRP * i + j
                if not last_:
                    pe.wait_ge(xe_ld[j], 16 * i + 16)
                    if not (first and j < 2):
                        pe.wait_ge(a_xeT, s - 1)
                    for k in range(HC):
                        last = nc.tensor.transpose(bank[j % 2][:, k * CAP:(k + 1) * CAP], xe[:, j, k * P:(k + 1) * P], ident)
                    last.then_inc(p_xeT, 1)
                if not (first and j < 1) and not (last_ and j > 0):
                    q = (j - 1) % GRP
                    pe.wait_ge(a_xeT, s)
                    if not (first and j < 3):
                        pe.wait_ge(v_hid, s - 2)
                        pe.wait_ge(a_w, s - 2)
                    for k in range(HC):
                        last = mm(bank[2 + q % 2][:, 0:GU + 1], xeT[:, q % 2, k * CAP:(k + 1) * CAP],
                                  expert_w[:, s - 1, k * (GU + 1):(k + 1) * (GU + 1)], start=k == 0, stop=k == HC - 1)
                    last.then_inc(p_gu, 1)
                if not (first and j < 2) and not (last_ and j > 1):
                    q = (j - 2) % GRP
                    pe.wait_ge(v_hid, s - 1)
                    if not (first and j < 4):
                        pe.wait_ge(a_hidT, s - 3)
                    nc.tensor.transpose(bank[4 + q % 2][0:I, 0:CAP], hid[:, q % 2, :], ident).then_inc(p_hidT, 1)
                if not (first and j < 3):
                    q = (j - 3) % GRP
                    pe.wait_ge(a_hidT, s - 2)
                    if not (first and j < 5):
                        pe.wait_ge(v_ye, s - 4)
                    mm(bank[6 + q % 2][:, 0:H], hidT[:, q % 2, :], expert_w[0:I, s - 3, HC * (GU + 1):EW],
                       start=True, stop=True).then_inc(p_ye, 1)

            for j in range(GRP):
                expert_steps(0, j, True, False)
            with pe.Fori(1, EARLY // GRP) as i:
                for j in range(GRP):
                    expert_steps(i, j, False, False)
            pe.wait_ge(s_lw, 16 * 3 * (E - EARLY) // GRP)
            pe.wait_ge(g_rcol, 2 * HC)
            with pe.Fori(EARLY // GRP, E // GRP) as i:
                for j in range(GRP):
                    expert_steps(i, j, False, False)
            for j in range(3):
                expert_steps(E // GRP, j, False, True)

        @block.vector
        def _(dve):
            link, clear = linker(dve, vch)
            V = nc.vector
            dve.wait_ge(s_c, 64)
            dve.wait_ge(a_econd, 1)
            link(V.tensor_scalar(cond_sb[:, 2, :], cond_sb[:, 1, :], 1.0, None, ALU.add))
            link(V.reciprocal(cond_sb[:, 1, :], cond_sb[:, 2, :]))
            V.tensor_tensor(cond_sb[:, 3, :], cond_sb[:, 0, :], cond_sb[:, 1, :], ALU.mult).then_inc(v_silu, 1)
            link(V.memset(onesb, 1.0))
            link(V.memset(ones3, 1.0))
            link(V.memset(seen[:, :, :], 0.0))
            link(V.memset(v_aug, 0.0))
            link(V.memset(v_aug[:, :, :, D:D + 1], 1.0))
            link(V.memset(neg3[:, :, :, :, :], 0.0))
            link(V.tensor_copy(ident16, ident))
            link(V.tensor_copy(identb, ident))
            link(V.tensor_copy(maskb, cst[:, P:2 * P]))
            link(V.tensor_copy(maskTb, cst[:, 2 * P:3 * P]))
            link(V.tensor_copy(prefixb, cst[:, 3 * P:4 * P]))
            dve.wait_ge(p_condT, 1)
            V.tensor_copy(condT[:, :, :], bank[0][:, 0:HC * B].rearrange("p (k b) -> p k b", b=B)).then_inc(v_condT, 1)
            V.tensor_copy(pickb[:, :, :], cst[:, 4 * P:4 * P + NH, None].broadcast_to([P, NH, P])).then_inc(v_csts, 1)
            dve.wait_ge(s_x, 16)
            for n in range(B * TPB):
                link(V.bn_stats(stats[:, n, :], x_sb[:, n, :]))
            for n in range(B * TPB):
                link(V.bn_aggr(mv1[:, n, :], stats[:, n, :]))
            V.tensor_scalar(rs1[:, 0, :], mv1[:, :, 1], EPS, None, ALU.add).then_inc(v_var1, 1)
            dve.wait_ge(p_mod, 1)
            for n in range(3):
                link(V.tensor_copy(mod_sb[:, n * 512:(n + 1) * 512], bank[1 + n][0:B, :]))
            for n in (1, 4):
                link(V.tensor_scalar(mod_sb[:, n * H:(n + 1) * H], mod_sb[:, n * H:(n + 1) * H], 1.0, None, ALU.add))
            for n in (2, 5):
                g = mod_sb[:, n * H:(n + 1) * H]
                link(V.tensor_scalar(mod_t[:, 0, :], g, 0.0, 2.0, ALU.is_ge, ALU.mult))
                link(V.tensor_scalar(mod_t[:, 0, :], mod_t[:, 0, :], 1.0, None, ALU.subtract))
                link(V.scalar_tensor_tensor(mod_t[:, 1, :], g, -1.0, g, ALU.mult, ALU.max))
                ins = V.scalar_tensor_tensor(g, mod_t[:, 1, :], 0.25, mod_t[:, 0, :], ALU.max, ALU.mult)
                if n == 2:
                    link(ins)
                else:
                    ins.then_inc(v_mod, 1)
            dve.wait_ge(p_modT, 1)
            V.tensor_copy(modT[:, :, :], bank[4][:, 0:4 * B].rearrange("p (n b) -> p n b", b=B)).then_inc(v_modT, 1)

            def refine(rs):
                link(V.tensor_tensor(rs[:, 1, :], rs[:, 2, :], rs[:, 2, :], ALU.mult))
                link(V.tensor_tensor(rs[:, 1, :], rs[:, 1, :], rs[:, 0, :], ALU.mult))
                link(V.tensor_scalar(rs[:, 1, :], rs[:, 1, :], -0.5, 1.5, ALU.mult, ALU.add))
                link(V.tensor_tensor(rs[:, 3, :], rs[:, 1, :], rs[:, 2, :], ALU.mult))

            dve.wait_ge(a_rs1, 1)
            refine(rs1)

            def normalise(it):
                for t in range(TPB):
                    n = TPB * it + t
                    ins = V.tensor_scalar(xn[:, t, :], x_sb[:, n, :], mv1[:, n, 0:1], rs1[:, 3, bass.ts(n, 1)],
                                          ALU.subtract, ALU.mult)
                    if t == TPB - 1:
                        ins.then_inc(v_xn, 1)
                    else:
                        link(ins)

            def rope_tile(it, t):
                dve.wait_ge(p_qkv, TPB * it + t + 1)
                qk = bank[1 + t][:, :]
                pairs = qk.rearrange("p (m i two) -> p m i two", i=D // 2, two=2)
                r2 = rope2.rearrange("p (m i two) -> p m i two", i=D // 2, two=2)
                heads = 2 * NH
                cos = rope_sb[:, t, 0, None, :].broadcast_to([P, heads, D])
                sin = rope_sb[:, t, 1, :].rearrange("p (i two) -> p i two", two=2)
                link(V.tensor_tensor(rope1.rearrange("p (m d) -> p m d", d=D), qk.rearrange("p (m d) -> p m d", d=D), cos, ALU.mult))
                for o in range(2):
                    link(V.tensor_tensor(r2[:, :, :, o], pairs[:, :, :, 1 - o],
                                         sin[:, None, :, o].broadcast_to([P, heads, D // 2]), ALU.mult))
                V.tensor_tensor(rope1, rope1, rope2, ALU.add).then_inc(v_rope, 1)
                dve.wait_ge(v_rope, TPB * it + t + 1)
                dve.wait_ge(a_hi, 2 * (TPB * it + t + 1))
                link(V.tensor_tensor(q_split[:, t, :, 2, :], rope1[:, 0:H].rearrange("p (h d) -> p h d", d=D),
                                     q_split[:, t, :, 0, :], ALU.subtract))
                link(V.tensor_tensor(k_split[:, t, :, 1, :], rope1[:, H:2 * H].rearrange("p (h d) -> p h d", d=D),
                                     k_split[:, t, :, 0, :], ALU.subtract))
                for o in range(2):
                    link(V.tensor_copy(q_split[:, t, :, 2 * o + 1, :], q_split[:, t, :, 2 * o, :]))
                V.tensor_copy(k_split[:, t, :, 2:4, :], k_split[:, t, :, 0:2, :]).then_inc(v_split, 1)

            def q_copy(it, t):
                dve.wait_ge(p_qkT, 4 * it + 2 * t + 1)
                src = bank16[(1, 3)[t]].rearrange("p (g q) -> p g q", q=P)
                V.tensor_copy(qT[:, :, t * P:(t + 1) * P], src).then_inc(v_qT, 1)

            def mid(it, b):
                rope_tile(it, 0)
                rope_tile(it, 1)
                if b is not None:
                    dve.wait_ge(p_pv, 4 * (b + 1))
                V.tensor_copy(v_aug[:, :, :, 0:D],
                              bank[3][:, :].rearrange("p (t h d) -> p t h d", t=TPB, h=NH)).then_inc(v_vaug, 1)
                q_copy(it, 0)
                q_copy(it, 1)

            def maxima(it):
                n = 0
                for g in range(4):
                    par, half = g // 2, g % 2
                    for i0, nh, qt in ((0, 4, 0), (0, 2, 1), (2, 2, 1)):
                        dve.wait_ge(p_s1, 12 * it + n + 1)
                        w = (qt + 1) * P
                        src = bank[4 + n % 3][:, 0:nh * w].rearrange("p (h k) -> p h k", k=w)
                        h0 = par + 8 * half + 2 * i0
                        V.tensor_reduce(rmax[:, qt, h0:h0 + 2 * nh - 1:2], src, AX.X, ALU.max).then_inc(v_max, 1)
                        n += 1

            def split_maxima(it):
                dve.wait_ge(v_max, 12 * (it + 1))
                link(V.tensor_scalar(negr[:, 0, :, :], rmax[:, :, :], -1.0, None, ALU.mult))
                for part in range(3):
                    src = negr[:, part % 2, :, :]
                    link(V.tensor_copy(neg3[:, :, 0, part, :], src))
                    if part < 2:
                        link(V.tensor_tensor(negr[:, 1 - part % 2, :, :], src, neg3[:, :, 0, part, :], ALU.subtract))
                V.tensor_copy(neg3[:, :, 1, 0:3, :], neg3[:, :, 0, 0:3, :]).then_inc(v_neg, 1)

            def back(b):
                for t in range(TPB):
                    dve.wait_ge(p_attq, TPB * b + t + 1)
                    src = bank[1 + t][:, :].rearrange("p (m c) -> p m c", c=32)
                    link(V.reciprocal(rden[:, t, :], src[:, :, D]))
                    dst = att_tok[:, t, :].rearrange("p (m par d) -> p par m d", par=2, d=D)
                    V.tensor_tensor(dst, src[:, :, 0:D].rearrange("p (par m) d -> p par m d", par=2),
                                    rden[:, t, :].rearrange("p (par m o) -> p par m o", par=2, o=1).broadcast_to([P, 2, NH // 2, D]),
                                    ALU.mult).then_inc(v_att, 1)
                dve.wait_ge(p_o, b + 1)
                dve.wait_ge(s_mb, 32)
                if not isinstance(b, int) or b > 0:
                    dve.wait_ge(g_scat, 16 * K * TPB * b)
                xb = x_sb[:, bass.ts(b, TPB), :]
                r2 = rope2_view

                def mrow(n):
                    return modB[:, bass.ts(b, 1), n * H:(n + 1) * H].broadcast_to([P, TPB, H])

                link(V.tensor_tensor(r2, bank[3][:, :].rearrange("p (t h) -> p t h", t=TPB), mrow(0), ALU.mult))
                link(V.tensor_tensor(xb, xb, r2, ALU.add))
                for t in range(TPB):
                    link(V.bn_stats(stats[:, t, :], x_sb[:, TPB * b + t, :]))
                for t in range(TPB):
                    link(V.bn_aggr(mv2[:, t, :], stats[:, t, :]))
                V.tensor_scalar(rs2[:, 0, :], mv2[:, :, 1], EPS, None, ALU.add).then_inc(v_x2, 1)
                dve.wait_ge(a_rs2, b + 1)
                refine(rs2)
                for t in range(TPB):
                    link(V.tensor_scalar(r2[:, t, :], x_sb[:, TPB * b + t, :], mv2[:, t, 0:1], rs2[:, 3, t:t + 1],
                                         ALU.subtract, ALU.mult))
                link(V.tensor_tensor(r2, r2, mrow(2), ALU.mult))
                V.tensor_tensor(rows[:, :, 0:H], r2, mrow(1), ALU.add).then_inc(v_h2, 1)
                dve.wait_ge(p_log, b + 1)
                link(V.tensor_copy(logit[:, :, :], bank[1][:, 0:TPB * E].rearrange("p (t e) -> p t e", t=TPB)))
                for t in range(TPB):
                    link(V.max(top8[:, t, :], logit[:, t, :]))
                V.tensor_scalar(rows[:, :, H:H + 1], top8[:, :, 0:1], -1.0, None, ALU.mult).then_inc(v_top, 1)
                for t in range(TPB):
                    link(V.match_replace(logit_rep[:, t, :], top8[:, t, :], logit[:, t, :], FAR))
                link(V.tensor_tensor(sel[:, :, :], logit[:, :, :], logit_rep[:, :, :], ALU.not_equal))
                for t in range(TPB - 1):
                    link(V.tensor_tensor(seen[:, t + 1, :], seen[:, t, :], sel[:, t, :], ALU.add))
                dve.wait_ge(vch, n_chain())
                V.tensor_copy(code[:, 0, :, :], sel[:, :, :]).then_inc(v_sel, 1)
                dve.wait_ge(p_cum, b + 1)
                rank = bank[2][:, 0:TPB * E].rearrange("p (t e) -> p t e", t=TPB)
                link(V.scalar_tensor_tensor(code[:, 0, :, :], rank, float(CAP), sel[:, :, :], ALU.is_le, ALU.mult))
                base = cst[:, None, 4 * P + NH:4 * P + NH + E].broadcast_to([P, TPB, E])
                link(V.scalar_tensor_tensor(code[:, 1, :, :], rank, -1.0, base, ALU.mult, ALU.add))
                link(V.tensor_tensor(code[:, 0, :, :], code[:, 0, :, :], code[:, 1, :, :], ALU.mult))
                link(V.tensor_tensor(seen[:, 0, :], seen[:, TPB - 1, :], sel[:, TPB - 1, :], ALU.add))
                for t in range(TPB):
                    link(V.max(code8[:, t, :], code[:, 0, t, :]))
                dve.wait_ge(a_sum, TPB * (b + 1))
                link(V.reciprocal(rows[:, :, H + 1], sum8[:, :]))
                link(V.tensor_copy(rows[:, :, H + 2:H + 3].bitcast(I32),
                                   tok[:, bass.ts(b, TPB)].rearrange("p (t o) -> p t o", o=1)))
                for t in range(TPB):
                    V.tensor_scalar(slot_idx[:, t, :], code8[:, t, :], -1.0, float(BIGSLOT), ALU.mult, ALU.add).then_inc(v_slot, 1)

            def n_chain():
                return chain_count[0]

            chain_count = [0]
            plain_link, plain_clear = link, clear

            def link(ins):
                chain_count[0] += 1
                plain_link(ins)

            def clear():
                chain_count[0] = 0
                plain_clear()

            dve.wait_ge(s_md, 16)
            rope2_view = rope2.rearrange("p (t h) -> p t h", t=TPB)
            normalise(0)
            mid(0, None)
            maxima(0)
            split_maxima(0)
            with dve.Fori(1, B) as it:
                clear()
                normalise(it)
                mid(it, it - 1)
                maxima(it)
                back(it - 1)
                split_maxima(it)
            clear()
            back(B - 1)

            def expert_steps(i, j, first, last_):
                s = GRP * i + j
                if not (first and j < 1) and not (last_ and j > 0):
                    q = (j - 1) % GRP
                    gu = bank[2 + q % 2]
                    dve.wait_ge(a_w, s)
                    if not (first and j < 3):
                        dve.wait_ge(p_hidT, s - 2)
                    link(V.tensor_scalar(hid0[:, q % 2, :], expg[:, q % 2, :], 1.0, None, ALU.add))
                    link(V.reciprocal(expg[:, q % 2, :], hid0[:, q % 2, :]))
                    link(V.tensor_tensor(hid0[:, q % 2, :], gu[:, 0:I], expg[:, q % 2, :], ALU.mult))
                    V.tensor_tensor(hid[:, q % 2, :], hid0[:, q % 2, :], gu[:, I:GU], ALU.mult).then_inc(v_hid, 1)
                if not (first and j < 3):
                    q = (j - 3) % GRP
                    dve.wait_ge(p_ye, s - 2)
                    dve.wait_ge(a_w, s - 2)
                    if not (first and j < 3 + NACC):
                        dve.wait_ge(added[q % NACC], 16 * (2 * i + (-1 if j < 3 else (j - 3) // NACC)))
                    V.tensor_scalar(ye[:, q % NACC, :], bank[6 + q % 2][:, 0:H], gatew[:, q:q + 1], xe[:, q, H + 1:H + 2],
                                    ALU.mult, ALU.mult).then_inc(v_ye, 1)

            clear()
            for j in range(GRP):
                expert_steps(0, j, True, False)
            with dve.Fori(1, E // GRP) as i:
                clear()
                for j in range(GRP):
                    expert_steps(i, j, False, False)
            clear()
            for j in range(3):
                expert_steps(E // GRP, j, False, True)

            dve.wait_ge(sum_ld, 16 * NACC)
            part = [arena[:, a * TOK * 2:(a + 1) * TOK * 2].rearrange("p (n h) -> p n h", h=H) for a in range(NACC)]
            for b in range(B):
                ts = slice(TPB * b, TPB * b + TPB)
                link(V.tensor_tensor(part[0][:, ts, :], part[0][:, ts, :], part[1][:, ts, :], ALU.add))
                link(V.tensor_tensor(part[2][:, ts, :], part[2][:, ts, :], part[3][:, ts, :], ALU.add))
                link(V.tensor_tensor(part[0][:, ts, :], part[0][:, ts, :], part[2][:, ts, :], ALU.add))
                link(V.tensor_tensor(part[0][:, ts, :], part[0][:, ts, :],
                                     gbB[:, bass.ts(b, 1), :].broadcast_to([P, TPB, H]), ALU.mult))
                V.tensor_tensor(x_sb[:, ts, :], x_sb[:, ts, :], part[0][:, ts, :], ALU.add).then_inc(v_out, 1)


def kernel(**inputs):
    import numpy as np
    import concourse.bacc as bacc
    from concourse.bass_utils import run_bass_kernel_spmd

    a = {n.removeprefix("L0_"): np.asarray(v) for n, v in inputs.items()}
    f32 = np.float32
    B, S, H = a["attn_x"].shape
    D, P, E, CAP = 16, 128, a["ffn_router_weight"].shape[0], 128
    half = D // 2
    inv = (1.0 / np.float32(10000.0) ** (np.arange(half, dtype=f32) / f32(half))).astype(f32)
    ang = np.arange(S, dtype=f32)[:, None] * inv[None, :]
    cos = np.repeat(np.cos(ang), 2, axis=-1)
    sin = np.repeat(np.sin(ang), 2, axis=-1)
    sin[:, 0::2] *= -1
    rope = np.stack([cos, sin], 1).astype(f32)
    r = np.arange(P)
    consts = np.concatenate([
        np.eye(P),
        np.where(r[None, :] <= r[:, None], 0.0, -1e30),
        np.where(r[None, :] >= r[:, None], 0.0, -1e30),
        r[:, None] <= r[None, :],
        (r[:, None] % 64 % 16 == np.arange(16)[None, :]) & (r[:, None] % 64 < 48),
        np.broadcast_to(2 * E * CAP + 1 - CAP * np.arange(E), (P, E)),
    ], 1).astype(f32)
    token_ids = (r[:, None] + P * np.arange(B * S // P + 1)[None, :]).astype(np.int32)
    arrays = {
        "x": a["attn_x"],
        "wqkvT": np.ascontiguousarray(np.concatenate([a["attn_Wq"], a["attn_Wk"], a["attn_Wv"]], 0).T),
        "bias": np.concatenate([a["attn_bq"], a["attn_bk"], a["attn_bv"], a["attn_bo"]])[None, :],
        "woT": np.ascontiguousarray(a["attn_Wo"].T),
        "routerT": np.ascontiguousarray(a["ffn_router_weight"].T),
        "gate_up": a["ffn_gate_up_proj"],
        "down": a["ffn_down_proj"],
        "cond": a["c"],
        "wmod": a["wmod"],
        "rope": rope,
        "consts": consts,
        "token_ids": token_ids,
    }
    nc = bacc.Bacc("TRN2", target_bir_lowering=False, num_devices=1)
    args = [nc.dram_tensor(f"in_{n}", v.shape, mybir.dt.from_np(v.dtype), kind="ExternalInput").ap()
            for n, v in arrays.items()]
    args.append(nc.dram_tensor("out_y", (B, S, H), mybir.dt.float32, kind="ExternalOutput").ap())
    adaln_moe_program(nc, *args)
    got = run_bass_kernel_spmd(nc, [{f"in_{n}": v for n, v in arrays.items()}], core_ids=[0])
    return got.results[0]["out_y"]
```

```python
import concourse.bass as bass
from concourse import mybir
from contextlib import ExitStack


def adaln_moe_program(nc, x, wqkvT, bias, woT, routerT, gate_up, down, cond, wmod,
                      rope, consts, token_ids, out):
    FP32, BF16, FP16 = mybir.dt.float32, mybir.dt.bfloat16, mybir.dt.float16
    I32, U32 = mybir.dt.int32, mybir.dt.uint32
    ACT, ALU, AX = mybir.ActivationFunctionType, mybir.AluOpType, mybir.AxisListType

    B, S, H = x.shape
    P = 128
    TPB = S // P
    HC = H // P
    NH = 16
    D = H // NH
    E, _, GU = gate_up.shape
    I = GU // 2
    K = 8
    CAP = 128
    TOK = B * S
    SLOTS = E * CAP
    ROW = H + 4
    NACC = 4
    ACCROWS = TOK + CAP
    EW = HC * (GU + 1) + H
    EARLY = 32
    GRP = 8
    SCALE = 1.0 / float(D) ** 0.5
    EPS = 1e-5
    FAR = -3.0e38
    BIGSLOT = 2 * SLOTS

    slot_rows = nc.dram_tensor("slot_rows", [SLOTS, ROW], FP32, kind="Internal").ap()
    sums = [nc.dram_tensor(f"sum{a}", [ACCROWS, H], FP32, kind="Internal").ap() for a in range(NACC)]
    mod_dram = nc.dram_tensor("mod_rows", [B, 6 * H], FP32, kind="Internal").ap()

    ctx = ExitStack()
    with ctx:
        def sb(name, shape, dt=FP32):
            return ctx.enter_context(nc.sbuf_tensor(name, shape, dt))

        def sem(name):
            return ctx.enter_context(nc.semaphore(name))

        arena = sb("arena", [P, E * EW])
        x_sb = sb("x_sb", [P, B * TPB, H])
        gbB = sb("gbB", [P, B, H])
        rows = sb("rows", [P, TPB, ROW])
        cst = sb("cst", [P, 4 * P + NH + E])
        ident = cst[:, 0:P]
        tok = sb("tok", [P, B * TPB + 1], I32)
        router_sb = sb("router_sb", [P, HC, E])
        zero_row = sb("zero_row", [P, ROW])

        expert_w = arena[:, :].rearrange("p (e w) -> p e w", w=EW)

        NXE = 8
        stage = sb("stage", [P, NXE * (ROW + 1) + 2 * HC * CAP + 6 * I + 2 * CAP + NACC * H])

        def region(whole, at, limit):
            cur = [at]

            def take(shape, dt=FP32, parts=P):
                n = 1
                for d in shape:
                    n *= d
                w = n * (2 if dt in (BF16, FP16) else 4) // 4
                v = whole[0:parts, cur[0]:cur[0] + w]
                cur[0] += w
                assert cur[0] <= limit
                v = v if dt == FP32 else v.bitcast(dt)
                names = "abcde"[:len(shape)]
                if len(shape) == 1:
                    return v
                return v.rearrange("p (" + " ".join(names) + ") -> p " + " ".join(names), **dict(zip(names, shape)))
            return take

        ffn = region(stage, 0, stage.shape[1])
        xe = ffn([NXE, ROW])
        xeT = ffn([2, HC * CAP])
        tanhg = ffn([2, I])
        hid0 = ffn([2, I])
        hid = ffn([2, I])
        hidT = ffn([2, CAP], parts=I)
        gatew = ffn([NXE])
        ye = ffn([NACC, H])

        SC = TPB * S - P
        scratch = region(arena, EARLY * EW, E * EW)
        probT = scratch([2, 4 * SC])
        v_aug = scratch([TPB, NH, 32])
        qT = scratch([NH // 2, S], FP16)
        kT = scratch([NH // 2, S], FP16)
        h1T = scratch([HC, S])
        xn = scratch([TPB, H])
        rope1 = scratch([TPB, 2 * H])
        rope2 = scratch([2 * H])
        q_split = scratch([TPB, NH, 4, D], FP16)
        k_split = scratch([TPB, NH, 4, D], FP16)
        att_sb = scratch([2, 512])
        att_tok = scratch([TPB, H])
        attT = scratch([HC, S])
        wqkv_sb = scratch([HC, 3 * H])
        wo_sb = scratch([HC, H])
        modB = scratch([B, 3 * H])
        h2T = scratch([HC, S])
        mod_sb = scratch([6 * H], parts=B)
        mod_t = scratch([2, H], parts=B)
        before = region(arena, EARLY * EW, EARLY * EW + 2 * 4 * SC)
        wmod_sb = before([HC, 6 * H])
        at = EARLY * EW + 2 * 4 * SC + TPB * NH * 32
        before = region(arena, at, at + NH * S)
        bias_p = before([3, 4 * H], BF16, parts=1)
        at += NH * S // 2 + HC * S + TPB * H + (TPB + 1) * 2 * H + TPB * NH * 4 * D
        before = region(arena, at, at + 8 * H)
        bias_f = before([2, 4 * H], parts=1)

        early = region(stage, 0, stage.shape[1])
        rope_sb = sb("rope_sb", [P, TPB, 2, D])
        ident16 = early([P], FP16)
        identb = early([P], BF16)
        maskb = early([P], BF16)
        maskTb = early([P], BF16)
        prefixb = early([P], BF16)
        onesb = early([P], BF16)
        pickb = early([NH, P], BF16)
        ones3 = early([P], BF16, parts=3)
        bias3 = early([4 * H], BF16, parts=3)
        condT = sb("condT", [P, 4, HC, B])
        modT = sb("modT", [P, 4, B])
        stats = sb("stats", [P, B * TPB, 6])
        mv1 = sb("mv1", [P, B * TPB, 2])
        rs1 = sb("rs1", [P, 4, B * TPB])
        mv2 = sb("mv2", [P, TPB, 2])
        rs2 = sb("rs2", [P, 4, TPB])
        rmax = sb("rmax", [P, TPB, NH])
        negr = early([2, TPB, NH])
        neg3 = early([TPB, 2, 4, NH], BF16)
        negT = early([S], BF16)
        rden = sb("rden", [P, TPB, NH])
        logit = early([TPB, E])
        logit_rep = early([TPB, E])
        top8 = sb("top8", [P, TPB, K])
        exp8 = sb("exp8", [P, TPB, K])
        sum8 = sb("sum8", [P, TPB])
        sel = early([TPB, E], BF16)
        seen = early([TPB + 1, E], BF16)
        code = early([2, TPB, E])
        code8 = sb("code8", [P, TPB, K])
        slot_idx = sb("slot_idx", [P, TPB, K], U32)

        bank = [ctx.enter_context(nc.psum_tensor(f"bank{i}", [P, 512], FP32)) for i in range(8)]
        bank16 = [b[:, :].bitcast(FP16) for b in bank]
        bankb = [b[:, :].bitcast(BF16) for b in bank]

        s_c = sem("consts_loaded")
        s_m = sem("wmod_loaded")
        s_x0 = sem("first_x_loaded")
        s_x = sem("x_loaded")
        s_w2 = sem("wo_and_router_loaded")
        s_w = sem("attn_weights_loaded")
        s_bias = sem("bias_loaded")
        s_b3 = sem("bias3_moved")
        s_md = sem("mod_stored")
        s_mb = sem("mod_broadcast")
        s_ew = sem("early_experts_loaded")
        s_lw = [sem(f"late_experts_loaded{n}") for n in range(2)]
        s_fill = sem("slots_filled")
        s_zero = sem("zero_row_ready")
        vch = sem("vector_chain")
        ach = sem("scalar_chain")
        gch = sem("gpsimd_chain")
        v_csts = sem("consts_converted")
        s_ct = sem("cond_loaded")
        s_m0 = sem("wmod_front_loaded")
        a_tanh = sem("tanh_cond")
        v_silu = sem("silu_ready")
        p_mod = sem("mod_in_banks")
        v_mod = sem("mod_ready")
        p_modT = sem("modT_in_bank")
        v_modT = sem("modT_ready")
        g_bias = sem("bias_split")
        v_var1 = sem("variance1_ready")
        a_rs1 = sem("rstd1_guess")
        v_xn = sem("xn_ready")
        p_xnT = sem("xnT_in_bank")
        a_h1T = sem("h1T_ready")
        p_qkv = sem("qkv_in_banks")
        v_rope = sem("rope_ready")
        a_hi = sem("high_parts_ready")
        v_split = sem("split_ready")
        a_vaug = sem("v_ready")
        p_qkT = sem("qkT_in_banks")
        v_qT = sem("qT_ready")
        a_kT = sem("kT_ready")
        p_s1 = sem("scores_for_max")
        v_max = sem("max_taken")
        v_neg = sem("neg_max_split")
        p_negT = sem("neg_max_T")
        a_negT = sem("neg_max_T_ready")
        p_s2 = sem("scoresT_in_bank")
        a_exp = sem("probs_ready")
        p_pv = sem("pv_done")
        a_att = sem("att_copied")
        p_attq = sem("att_token_major")
        v_att = sem("att_normalised")
        p_attT = sem("attT_in_bank")
        a_attT = sem("attT_ready")
        p_o = sem("o_proj_done")
        v_x2 = sem("x2_variance")
        a_rs2 = sem("rstd2_guess")
        v_h2 = sem("h2_ready")
        p_h2T = sem("h2T_in_bank")
        a_h2T = sem("h2T_ready")
        p_log = sem("logits_in_bank")
        v_top = sem("top8_ready")
        a_sum = sem("sum8_ready")
        v_sel = sem("picks_ready")
        p_cum = sem("ranks_in_bank")
        v_rank = sem("ranks_bank_free")
        v_slot = sem("slots_ready")
        g_free = sem("rows_free")
        g_scat = sem("rows_scattered")
        g_rcol = sem("router_columns")
        xe_ld = [sem(f"slot_rows_loaded{j}") for j in range(NXE)]
        p_xeT = sem("xeT_in_bank")
        a_xeT = sem("xeT_ready")
        p_gu = sem("gate_up_in_bank")
        a_tg = sem("tanh_gate_ready")
        a_w = sem("gate_weight_ready")
        v_hid = sem("hidden_ready")
        p_hidT = sem("hiddenT_in_bank")
        a_hidT = sem("hiddenT_ready")
        p_ye = sem("expert_out_in_bank")
        v_ye = sem("expert_out_ready")
        added = [sem(f"added{a}") for a in range(NACC)]
        sum_ld = sem("sums_loaded")
        v_out = sem("out_ready")
        s_out = sem("out_stored")

        groups = [[par + 8 * half + 2 * i for i in range(4)] for par in range(2) for half in range(2)]
        row0 = [64 * (g // 2) for g in range(4)]

        def rope_part(t, n):
            return (rope1[:, t, n * H:(n + 1) * H].rearrange("p (h o d) -> p h o d", h=NH, o=1)
                    .broadcast_to([P, NH, 2, D]))

        block = ctx.enter_context(nc.Block())

        def linker(eng, chain):
            n = [0]

            def link(ins):
                n[0] += 1
                ins.then_inc(chain, 1)
                eng.wait_ge(chain, n[0])

            def clear():
                eng.sem_clear(chain)
                n[0] = 0
            return link, clear

        @block.sync
        def _(sp):
            wm = wmod.rearrange("(k p) n -> p k n", p=P)
            xr = x.rearrange("b (t p) h -> p (b t) h", p=P)
            sp.dma_start(condT[:, 0, :, :], cond).then_inc(s_ct, 16)
            sp.dma_start(bias_f[0:1, 0, :], bias).then_inc(s_bias, 16)
            sp.dma_start(wmod_sb[:, :, 0:2 * H], wm[:, :, 0:2 * H]).then_inc(s_m0, 16)
            sp.dma_start(x_sb[:, 0:TPB, :], xr[:, 0:TPB, :]).then_inc(s_x0, 16)
            sp.dma_start(cst[:, :], consts).then_inc(s_c, 16)
            sp.dma_start(tok[:, :], token_ids).then_inc(s_c, 16)
            sp.dma_start(rope_sb[:, :, :, :], rope.rearrange("(t p) a d -> p t a d", p=P)).then_inc(s_c, 16)
            sp.dma_start(wqkv_sb, wqkvT.rearrange("(k p) n -> p k n", p=P)).then_inc(s_w, 16)
            sp.dma_start(x_sb[:, TPB:, :], xr[:, TPB:, :]).then_inc(s_x, 16)
            sp.dma_start(wmod_sb[:, :, 2 * H:], wm[:, :, 2 * H:]).then_inc(s_m, 16)
            sp.dma_start(wo_sb, woT.rearrange("(k p) n -> p k n", p=P)).then_inc(s_w2, 16)
            sp.dma_start(router_sb[:, :, :], routerT.rearrange("(k p) n -> p k n", p=P)).then_inc(s_w2, 16)
            sp.wait_ge(g_bias, 1)
            sp.dma_start(bias3, bias_p[0:1, :, :]).then_inc(s_b3, 16)

            def load_experts(e0, s):
                e1 = e0 + GRP
                for k in range(HC):
                    sp.dma_start(expert_w[:, e0:e1, k * (GU + 1):k * (GU + 1) + GU],
                                 gate_up[e0:e1, k * P:(k + 1) * P, :].rearrange("e p f -> p e f")).then_inc(s, 16)
                sp.dma_start(expert_w[0:I, e0:e1, HC * (GU + 1):EW],
                             down[e0:e1, :, :].rearrange("e i h -> i e h")).then_inc(s, 16)

            sp.wait_ge(s_zero, 1)

            def fill_slots(n):
                sp.dma_start(slot_rows[n * 1024:(n + 1) * 1024, :].rearrange("(e c) r -> c e r", c=CAP),
                             zero_row[:, None, :].broadcast_to([P, 8, ROW])).then_inc(s_fill, 16)

            for n in range(2):
                fill_slots(n)
            sp.wait_ge(v_mod, 1)
            sp.dma_start(mod_dram[:, 2 * H:], mod_sb[:, 2 * H:]).then_inc(s_md, 16)
            sp.wait_ge(s_md, 16)
            sp.dma_start(modB, mod_dram[None, :, 2 * H:5 * H].broadcast_to([P, B, 3 * H])).then_inc(s_mb, 16)
            sp.dma_start(gbB[:, :, :], mod_dram[None, :, 5 * H:6 * H].broadcast_to([P, B, H])).then_inc(s_mb, 16)
            for n in range(2, 8):
                fill_slots(n)
            for a in range(NACC):
                sp.dma_start(sums[a].rearrange("(n p) h -> p n h", p=P),
                             zero_row[:, None, 0:H].broadcast_to([P, ACCROWS // P, H])).then_inc(s_fill, 16)
            for e0 in range(0, EARLY, GRP):
                load_experts(e0, s_ew)
            sp.wait_ge(v_slot, B * TPB)
            late = list(range(EARLY, E, GRP))
            for e0 in late[:2]:
                load_experts(e0, s_lw[0])
            sp.wait_ge(g_scat, 16 * K * B * TPB)

            def load_slots(i, j, first):
                e = GRP * i + j
                if not first:
                    sp.wait_ge(added[j % NACC], 16 * (2 * i - 1 + j // NACC))
                sp.dma_start(xe[:, j, :], slot_rows.rearrange("(e c) r -> c e r", c=CAP)[:, e, :]).then_inc(xe_ld[j], 16)

            for j in range(GRP):
                load_slots(0, j, True)
            for e0 in late[2:]:
                load_experts(e0, s_lw[1])
            with sp.Fori(1, E // GRP) as i:
                for j in range(GRP):
                    load_slots(i, j, False)
            for a in range(NACC):
                sp.wait_ge(added[a], 16 * (E // NACC))
                sp.dma_start(arena[:, a * TOK * 2:(a + 1) * TOK * 2].rearrange("p (t h) -> p t h", h=H),
                             sums[a][0:TOK, :].rearrange("(t p) h -> p t h", p=P)).then_inc(sum_ld, 16)
            for b in range(B):
                sp.wait_ge(v_out, b + 1)
                sp.dma_start(out[b].rearrange("(t p) h -> p t h", p=P), x_sb[:, bass.ts(b, TPB), :]).then_inc(s_out, 16)
            sp.wait_ge(s_out, 16 * B)

        @block.gpsimd
        def _(pool):
            link, clear = linker(pool, gch)
            link(nc.gpsimd.memset(zero_row[:, :], 0.0))
            pool.wait_ge(s_c, 48)
            nc.gpsimd.tensor_copy(zero_row[:, H + 2:H + 3].bitcast(I32), tok[:, B * TPB:B * TPB + 1]).then_inc(s_zero, 1)
            nc.gpsimd.memset(rows[:, :, H + 3:H + 4], 0.0).then_inc(g_free, 1)
            pool.wait_ge(s_bias, 16)
            link(nc.gpsimd.tensor_copy(bias_p[0:1, 0, :], bias_f[0:1, 0, :]))
            link(nc.gpsimd.tensor_tensor(bias_f[0:1, 1, :], bias_f[0:1, 0, :], bias_p[0:1, 0, :], ALU.subtract))
            link(nc.gpsimd.tensor_copy(bias_p[0:1, 1, :], bias_f[0:1, 1, :]))
            link(nc.gpsimd.tensor_tensor(bias_f[0:1, 0, :], bias_f[0:1, 1, :], bias_p[0:1, 1, :], ALU.subtract))
            nc.gpsimd.tensor_copy(bias_p[0:1, 2, :], bias_f[0:1, 0, :]).then_inc(g_bias, 1)
            pool.wait_ge(s_w2, 32)

            def router_columns(e0, e1):
                for k in range(HC):
                    c = k * (GU + 1) + GU
                    nc.gpsimd.tensor_copy(expert_w[:, e0:e1, c:c + 1],
                                          router_sb[:, k, e0:e1].rearrange("p (e o) -> p e o", o=1)).then_inc(g_rcol, 1)

            router_columns(0, EARLY)
            pool.wait_ge(s_fill, 16 * (8 + NACC))

            def scatter(b):
                for t in range(TPB):
                    pool.wait_ge(v_slot, TPB * b + t + 1)
                    for k in range(K):
                        pool.indirect_dma_start(
                            slot_rows, bass.IndirectOffsetOnAxis(ap=slot_idx[:, t, k:k + 1], axis=0),
                            rows[:, t, :], None, bounds_check=SLOTS - 1, oob_is_err=False).then_inc(g_scat, 16)

            for b in range(B):
                scatter(b)
                pool.wait_ge(g_scat, 16 * K * (b + 1) * TPB)
                if b < B - 1:
                    nc.gpsimd.memset(rows[:, :, H + 3:H + 4], 0.0).then_inc(g_free, 1)
            router_columns(EARLY, E)

            def add_expert(i, j, first):
                e = GRP * i + j
                pool.wait_ge(v_ye, e + 1)
                if not (first and j < NACC):
                    pool.wait_ge(added[j % NACC], 16 * (2 * i + j // NACC))
                pool.indirect_dma_start(
                    sums[j % NACC], bass.IndirectOffsetOnAxis(ap=xe[:, j, H + 2:H + 3].bitcast(U32), axis=0),
                    ye[:, j % NACC, :], None, bounds_check=ACCROWS - 1, oob_is_err=True,
                    compute_op=ALU.add).then_inc(added[j % NACC], 16)

            for e in range(E):
                add_expert(e // GRP, e % GRP, e < GRP)

        @block.scalar
        def _(act):
            link, clear = linker(act, ach)
            act.wait_ge(s_ct, 16)
            nc.scalar.activation(condT[:, 1, :, :], condT[:, 0, :, :], ACT.Tanh, scale=0.5).then_inc(a_tanh, 1)
            nc.scalar.preload_act_table_set("natural_log_exp_and_others")

            def rstd_guess(rs):
                link(nc.scalar.activation(rs[:, 1, :], rs[:, 0, :], ACT.Ln))
                return nc.scalar.activation(rs[:, 2, :], rs[:, 1, :], ACT.Exp, scale=-0.5)

            act.wait_ge(v_var1, 1)
            rstd_guess(rs1[:, :, 0:TPB]).then_inc(a_rs1, 1)
            act.wait_ge(v_modT, 1)
            act.wait_ge(v_csts, 1)

            def front(it):
                act.wait_ge(p_xnT, it + 1)
                for k in range(HC):
                    nc.scalar.activation(h1T[:, k, :], bank[3][:, k * S:(k + 1) * S], ACT.Identity,
                                         bias=modT[:, k, bass.ts(it, 1)], scale=modT[:, 2 + k, bass.ts(it, 1)]).then_inc(a_h1T, 1)

            def high(it, t):
                act.wait_ge(v_rope, TPB * it + t + 1)
                nc.scalar.activation(q_split[:, t, :, 0:2, :], rope_part(t, 0), ACT.Copy).then_inc(a_hi, 1)
                nc.scalar.activation(k_split[:, t, :, 0::2, :], rope_part(t, 1), ACT.Copy).then_inc(a_hi, 1)

            def softmax(b, it):
                n = 0
                for g in range(4):
                    if g >= 2:
                        act.wait_ge(p_pv, 4 * b + g - 1)
                    for part in range(3):
                        act.wait_ge(p_s2, 12 * b + n + 1)
                        dst = probT[:, g % 2, part * 512:(part + 1) * 512]
                        nc.scalar.activation(dst, bank[4 + n % 3][:, :], ACT.Exp, scale=SCALE).then_inc(a_exp, 1)
                        n += 1
                    if it is not None and g in (1, 2):
                        high(it, g - 1)
                    if g % 2:
                        act.wait_ge(p_pv, 4 * b + g + 1)
                        nc.scalar.activation(att_sb[:, g // 2, :], bank[7][:, :], ACT.Copy).then_inc(a_att, 1)

            def v_copy(it):
                act.wait_ge(p_qkv, TPB * (it + 1))
                nc.scalar.activation(v_aug[:, :, :, 0:D], bank[3][:, :].rearrange("p (t h d) -> p t h d", t=TPB, h=NH),
                                     ACT.Copy).then_inc(a_vaug, 1)

            def k_copy(it, t):
                act.wait_ge(p_qkT, 4 * it + 2 * t + 2)
                src = bank16[(0, 3)[t]].rearrange("p (g q) -> p g q", q=P)
                nc.scalar.activation(kT[:, :, t * P:(t + 1) * P], src, ACT.Copy).then_inc(a_kT, 1)

            def att_copy(b):
                act.wait_ge(p_attT, b + 1)
                nc.scalar.activation(attT[:, :, :], bank[6][:, :].rearrange("p (k q) -> p k q", k=HC),
                                     ACT.Copy).then_inc(a_attT, 1)

            def back(b):
                act.wait_ge(v_x2, b + 1)
                rstd_guess(rs2).then_inc(a_rs2, 1)
                act.wait_ge(p_h2T, b + 1)
                nc.scalar.activation(h2T[:, :, :], bank[0][:, :].rearrange("p (k q) -> p k q", k=HC),
                                     ACT.Copy).then_inc(a_h2T, 1)
                act.wait_ge(v_top, b + 1)
                for t in range(TPB):
                    nc.scalar.activation(exp8[:, t, :], top8[:, t, :], ACT.Exp, bias=rows[:, t, H:H + 1],
                                         accum_out=sum8[:, t:t + 1]).then_inc(a_sum, 1)

            def negs(it):
                act.wait_ge(p_negT, it + 1)
                nc.scalar.activation(negT, bankb[0][:, 0:S], ACT.Copy).then_inc(a_negT, 1)

            front(0)
            act.wait_ge(v_var1, 2)
            rstd_guess(rs1[:, :, TPB:]).then_inc(a_rs1, 1)
            high(0, 0)
            high(0, 1)
            v_copy(0)
            k_copy(0, 0)
            k_copy(0, 1)
            front(1)
            negs(0)

            def one_round(it, more):
                softmax(it - 1, it)
                v_copy(it)
                k_copy(it, 0)
                att_copy(it - 1)
                k_copy(it, 1)
                if more:
                    front(it + 1)
                back(it - 1)
                negs(it)

            with act.Fori(1, B - 1) as it:
                clear()
                one_round(it, True)
            clear()
            one_round(B - 1, False)
            softmax(B - 1, None)
            att_copy(B - 1)
            back(B - 1)
            nc.scalar.preload_act_table_set("exp_and_others")

            def expert_steps(i, j, first, last):
                s = GRP * i + j
                if not last:
                    act.wait_ge(p_xeT, s + 1)
                    if not (first and j < 2):
                        act.wait_ge(p_gu, s - 1)
                    nc.scalar.activation(xeT[:, j % 2, :], bank[j % 2][:, 0:HC * CAP], ACT.Copy).then_inc(a_xeT, 1)
                if not (first and j < 1) and not (last and j > 0):
                    q = (j - 1) % GRP
                    act.wait_ge(p_gu, s)
                    if not (first and j < 3):
                        act.wait_ge(v_hid, s - 2)
                    nc.scalar.activation(tanhg[:, q % 2, :], bank[2 + q % 2][:, 0:I], ACT.Tanh, scale=0.5).then_inc(a_tg, 1)
                    if not (first and j < GRP + 1):
                        act.wait_ge(v_ye, s - GRP)
                    nc.scalar.activation(gatew[:, q:q + 1], bank[2 + q % 2][:, GU:GU + 1], ACT.Exp,
                                         bias=xe[:, q, H:H + 1]).then_inc(a_w, 1)
                if not (first and j < 2) and not (last and j > 1):
                    q = (j - 2) % GRP
                    act.wait_ge(p_hidT, s - 1)
                    if not (first and j < 4):
                        act.wait_ge(p_ye, s - 3)
                    nc.scalar.activation(hidT[:, q % 2, :], bank[4 + q % 2][0:I, 0:CAP], ACT.Copy).then_inc(a_hidT, 1)

            for j in range(GRP):
                expert_steps(0, j, True, False)
            with act.Fori(1, E // GRP) as i:
                for j in range(GRP):
                    expert_steps(i, j, False, False)
            for j in range(3):
                expert_steps(E // GRP, j, False, True)

        @block.tensor
        def _(pe):
            mm = nc.tensor.matmul
            pe.wait_ge(v_silu, 1)
            pe.wait_ge(s_m0, 16)
            for n in range(4):
                for k in range(HC):
                    last = mm(bank[4][:, n * B:(n + 1) * B], wmod_sb[:, k, n * P:(n + 1) * P], condT[:, 3, k, :],
                              start=k == 0, stop=k == HC - 1)
            last.then_inc(p_modT, 1)
            pe.wait_ge(v_csts, 1)

            def mod_rows():
                pe.wait_ge(s_m, 16)
                for n in range(1, 3):
                    for k in range(HC):
                        last = mm(bank[4 + n][0:B, :], condT[:, 3, k, :], wmod_sb[:, k, n * 512:(n + 1) * 512],
                                  start=k == 0, stop=k == HC - 1)
                last.then_inc(p_mod, 1)

            def front(it):
                pe.wait_ge(v_xn, it + 1)
                for t in range(TPB):
                    for k in range(HC):
                        last = nc.tensor.transpose(bank[3][:, k * S + t * P:k * S + (t + 1) * P],
                                                   xn[:, t, k * P:(k + 1) * P], ident)
                last.then_inc(p_xnT, 1)

            def qkv(it, t):
                pe.wait_ge(a_h1T, HC * (it + 1))
                for dst, c0, c1 in ((bank[1 + t][:, :], 0, 2 * H), (bank[3][:, t * H:(t + 1) * H], 2 * H, 3 * H)):
                    for k in range(HC):
                        mm(dst, h1T[:, k, t * P:(t + 1) * P], wqkv_sb[:, k, c0:c1], start=k == 0, stop=False)
                    last = mm(dst, ones3, bias3[:, c0:c1], start=False, stop=True)
                last.then_inc(p_qkv, 1)

            def split_transposes(it, t):
                pe.wait_ge(v_split, TPB * it + t + 1)
                if t == 1:
                    pe.wait_ge(a_vaug, it + 1)
                for src, bk in ((q_split, (1, 2)[t]), (k_split, (0, 3)[t])):
                    flat = src[:, t, :, :, :].rearrange("p h a c -> p (h a c)")
                    for g in range(NH // 2):
                        last = nc.tensor.transpose(bank16[bk][:, g * P:(g + 1) * P], flat[:, g * P:(g + 1) * P], ident16)
                    last.then_inc(p_qkT, 1)

            def scores_for_max(it, n0, n1, b):
                if n0 == 0:
                    pe.wait_ge(v_qT, TPB * (it + 1))
                    pe.wait_ge(a_kT, TPB * (it + 1))
                for n in range(n0, n1):
                    g, part = n // 3, n % 3
                    r = slice(row0[g], row0[g] + 64)
                    heads, qt = ((groups[g], 0), (groups[g][0:2], 1), (groups[g][2:4], 1))[part]
                    bk = bank[4 + n % 3]
                    if n >= 3:
                        pe.wait_ge(v_max, 12 * it + n - 2)
                    elif b is None and n == 1:
                        pe.wait_ge(v_mod, 1)
                    w = (qt + 1) * P
                    view = bk[:, 0:len(heads) * w].rearrange("p (h k) -> p h k", k=w)
                    mm(view[:, :, w - P:w], identb, maskb[:, None, :].broadcast_to([P, len(heads), P]),
                       start=True, stop=False, skip_group_check=True)
                    for i, h in enumerate(heads):
                        last = mm(view[:, i, :], qT[r, h // 2, qt * P:(qt + 1) * P], kT[r, h // 2, 0:w],
                                  start=False, stop=i == len(heads) - 1, skip_group_check=True)
                    last.then_inc(p_s1, 1)

            def neg_transposes(it):
                pe.wait_ge(v_neg, it + 1)
                for t in range(TPB):
                    last = nc.tensor.transpose(bankb[0][:, t * P:(t + 1) * P],
                                               neg3[:, t, :, :, :].rearrange("p a c h -> p (a c h)"), identb)
                last.then_inc(p_negT, 1)

            def attend(b):
                pe.wait_ge(a_negT, b + 1)
                n = 0

                def pv(g):
                    if g == 0:
                        pe.wait_ge(v_rank, b + 1)
                    pe.wait_ge(a_exp, 12 * b + 3 * g + 3)
                    if g == 2:
                        pe.wait_ge(a_att, 2 * b + 1)
                    for kt in range(TPB):
                        for i, h in enumerate(groups[g]):
                            c = (g % 2) * S
                            src = (probT[:, g % 2, i * S:(i + 1) * S] if kt == 0 else
                                   probT[:, g % 2, 4 * S + i * P:4 * S + (i + 1) * P])
                            last = mm(bank[7][32 * i:32 * i + 32, c + kt * P:c + S], v_aug[:, kt, h, :], src,
                                      start=kt == 0, stop=kt == TPB - 1, skip_group_check=True)
                    last.then_inc(p_pv, 1)

                for g in range(4):
                    r = slice(row0[g], row0[g] + 64)
                    rn = slice(row0[g], row0[g] + 48)
                    for heads, kt in ((groups[g][0:2], 0), (groups[g][2:4], 0), (groups[g], 1)):
                        bk = bank[4 + n % 3]
                        if n >= 3:
                            pe.wait_ge(a_exp, 12 * b + n - 2)
                        w = (TPB - kt) * P
                        view = bk[:, 0:len(heads) * w].rearrange("p (h q) -> p h q", q=w)
                        mm(view[:, :, 0:P], identb, maskTb[:, None, :].broadcast_to([P, len(heads), P]),
                           start=True, stop=False, skip_group_check=True)
                        for i, h in enumerate(heads):
                            mm(view[:, i, :], kT[r, h // 2, kt * P:(kt + 1) * P], qT[r, h // 2, kt * P:S],
                               start=False, stop=False, skip_group_check=True)
                            last = mm(view[:, i, :], pickb[rn, h, :], negT[rn, kt * P:S],
                                      start=False, stop=i == len(heads) - 1, skip_group_check=True)
                        last.then_inc(p_s2, 1)
                        n += 1
                    if g > 0:
                        pv(g - 1)
                pv(3)

            def att_transposes(b):
                pe.wait_ge(a_att, 2 * b + 2)
                for t in range(TPB):
                    for g in range(4):
                        last = nc.tensor.transpose(bank[4 + t][:, g * P:(g + 1) * P],
                                                   att_sb[:, g // 2, (g % 2) * S + t * P:(g % 2) * S + (t + 1) * P], ident)
                    last.then_inc(p_attq, 1)

            def o_proj(b):
                for t in range(TPB):
                    pe.wait_ge(v_att, TPB * b + t + 1)
                    for k in range(HC):
                        last = nc.tensor.transpose(bank[6][:, k * S + t * P:k * S + (t + 1) * P],
                                                   att_tok[:, t, k * P:(k + 1) * P], ident)
                last.then_inc(p_attT, 1)
                pe.wait_ge(a_attT, b + 1)
                for t in range(TPB):
                    dst = bank[7][:, t * H:(t + 1) * H]
                    for k in range(HC):
                        mm(dst, attT[:, k, t * P:(t + 1) * P], wo_sb[:, k, :], start=k == 0, stop=False)
                    last = mm(dst, ones3, bias3[:, 3 * H:4 * H], start=False, stop=True)
                last.then_inc(p_o, 1)

            def h2_transposes(b):
                pe.wait_ge(v_h2, b + 1)
                for t in range(TPB):
                    for k in range(HC):
                        last = nc.tensor.transpose(bank[0][:, k * S + t * P:k * S + (t + 1) * P],
                                                   rows[:, t, k * P:(k + 1) * P], ident)
                last.then_inc(p_h2T, 1)

            def router(b):
                pe.wait_ge(a_h2T, b + 1)
                for t in range(TPB):
                    for k in range(HC):
                        last = mm(bank[7][:, t * E:(t + 1) * E], h2T[:, k, t * P:(t + 1) * P], router_sb[:, k, :],
                                  start=k == 0, stop=k == HC - 1)
                last.then_inc(p_log, 1)

            def ranks(b):
                pe.wait_ge(v_sel, b + 1)
                for t in range(TPB):
                    dst = bank[7][:, 256 + t * E:256 + (t + 1) * E]
                    mm(dst, prefixb, sel[:, t, :], start=True, stop=False)
                    last = mm(dst, onesb, seen[:, t, :], start=False, stop=True)
                last.then_inc(p_cum, 1)

            def one_round(it, more):
                b = it - 1
                attend(b)
                split_transposes(it, 0)
                att_transposes(b)
                split_transposes(it, 1)
                o_proj(b)
                scores_for_max(it, 0, 3, b)
                if more:
                    front(it + 1)
                scores_for_max(it, 3, 5, b)
                if more:
                    qkv(it + 1, 0)
                scores_for_max(it, 5, 6, b)
                h2_transposes(b)
                if more:
                    qkv(it + 1, 1)
                scores_for_max(it, 6, 8, b)
                router(b)
                scores_for_max(it, 8, 12, b)
                ranks(b)
                neg_transposes(it)

            front(0)
            pe.wait_ge(s_w, 16)
            pe.wait_ge(s_b3, 16)
            qkv(0, 0)
            qkv(0, 1)
            mod_rows()
            pe.wait_ge(s_w2, 32)
            split_transposes(0, 0)
            split_transposes(0, 1)
            scores_for_max(0, 0, 3, None)
            front(1)
            scores_for_max(0, 3, 6, None)
            qkv(1, 0)
            scores_for_max(0, 6, 9, None)
            qkv(1, 1)
            scores_for_max(0, 9, 12, None)
            neg_transposes(0)
            with pe.Fori(1, B - 1) as it:
                one_round(it, True)
            one_round(B - 1, False)
            attend(B - 1)
            att_transposes(B - 1)
            o_proj(B - 1)
            h2_transposes(B - 1)
            router(B - 1)
            ranks(B - 1)

            pe.wait_ge(v_slot, TPB * B)
            pe.wait_ge(g_rcol, HC)
            pe.wait_ge(s_ew, 16 * 3 * EARLY // GRP)

            def expert_steps(i, j, first, last_):
                s = GRP * i + j
                if not last_:
                    pe.wait_ge(xe_ld[j], 16 * i + 16)
                    if not (first and j < 2):
                        pe.wait_ge(a_xeT, s - 1)
                    for k in range(HC):
                        last = nc.tensor.transpose(bank[j % 2][:, k * CAP:(k + 1) * CAP], xe[:, j, k * P:(k + 1) * P], ident)
                    last.then_inc(p_xeT, 1)
                if not (first and j < 1) and not (last_ and j > 0):
                    q = (j - 1) % GRP
                    pe.wait_ge(a_xeT, s)
                    if not (first and j < 3):
                        pe.wait_ge(v_hid, s - 2)
                        pe.wait_ge(a_w, s - 2)
                    for k in range(HC):
                        last = mm(bank[2 + q % 2][:, 0:GU + 1], xeT[:, q % 2, k * CAP:(k + 1) * CAP],
                                  expert_w[:, s - 1, k * (GU + 1):(k + 1) * (GU + 1)], start=k == 0, stop=k == HC - 1)
                    last.then_inc(p_gu, 1)
                if not (first and j < 2) and not (last_ and j > 1):
                    q = (j - 2) % GRP
                    pe.wait_ge(v_hid, s - 1)
                    if not (first and j < 4):
                        pe.wait_ge(a_hidT, s - 3)
                    nc.tensor.transpose(bank[4 + q % 2][0:I, 0:CAP], hid[:, q % 2, :], ident).then_inc(p_hidT, 1)
                if not (first and j < 3):
                    q = (j - 3) % GRP
                    pe.wait_ge(a_hidT, s - 2)
                    if not (first and j < 5):
                        pe.wait_ge(v_ye, s - 4)
                    mm(bank[6 + q % 2][:, 0:H], hidT[:, q % 2, :], expert_w[0:I, s - 3, HC * (GU + 1):EW],
                       start=True, stop=True).then_inc(p_ye, 1)

            for j in range(GRP):
                expert_steps(0, j, True, False)
            with pe.Fori(1, EARLY // GRP) as i:
                for j in range(GRP):
                    expert_steps(i, j, False, False)
            pe.wait_ge(g_rcol, 2 * HC)
            half = (E - EARLY) // GRP // 2
            for n in range(2):
                pe.wait_ge(s_lw[n], 16 * 3 * half)
                with pe.Fori(EARLY // GRP + n * half, EARLY // GRP + (n + 1) * half) as i:
                    for j in range(GRP):
                        expert_steps(i, j, False, False)
            for j in range(3):
                expert_steps(E // GRP, j, False, True)

        @block.vector
        def _(dve):
            link, clear = linker(dve, vch)
            V = nc.vector
            dve.wait_ge(a_tanh, 1)
            link(V.scalar_tensor_tensor(condT[:, 2, :, :], condT[:, 1, :, :], 1.0, condT[:, 0, :, :], ALU.add, ALU.mult))
            V.tensor_scalar(condT[:, 3, :, :], condT[:, 2, :, :], 0.5, None, ALU.mult).then_inc(v_silu, 1)

            def statistics(n0, n1):
                for n in range(n0, n1):
                    link(V.bn_stats(stats[:, n, :], x_sb[:, n, :]))
                for n in range(n0, n1):
                    link(V.bn_aggr(mv1[:, n, :], stats[:, n, :]))
                V.tensor_scalar(rs1[:, 0, n0:n1], mv1[:, n0:n1, 1], EPS, None, ALU.add).then_inc(v_var1, 1)

            def refine(rs):
                link(V.tensor_tensor(rs[:, 1, :], rs[:, 2, :], rs[:, 2, :], ALU.mult))
                link(V.tensor_tensor(rs[:, 1, :], rs[:, 1, :], rs[:, 0, :], ALU.mult))
                link(V.tensor_scalar(rs[:, 1, :], rs[:, 1, :], -0.5, 1.5, ALU.mult, ALU.add))
                link(V.tensor_tensor(rs[:, 3, :], rs[:, 1, :], rs[:, 2, :], ALU.mult))

            dve.wait_ge(s_x0, 16)
            statistics(0, TPB)
            dve.wait_ge(p_modT, 1)
            modv = bank[4][:, 0:4 * B].rearrange("p (n b) -> p n b", b=B)
            link(V.tensor_copy(modT[:, 0:2, :], modv[:, 0:2, :]))
            V.tensor_scalar(modT[:, 2:4, :], modv[:, 2:4, :], 1.0, None, ALU.add).then_inc(v_modT, 1)
            dve.wait_ge(s_c, 48)
            link(V.tensor_copy(ident16, ident))
            link(V.tensor_copy(identb, ident))
            link(V.tensor_copy(maskb, cst[:, P:2 * P]))
            link(V.tensor_copy(maskTb, cst[:, 2 * P:3 * P]))
            link(V.tensor_copy(prefixb, cst[:, 3 * P:4 * P]))
            link(V.memset(onesb, 1.0))
            link(V.memset(ones3, 1.0))
            link(V.memset(v_aug, 0.0))
            link(V.memset(v_aug[:, :, :, D:D + 1], 1.0))
            dve.wait_ge(a_rs1, 1)
            refine(rs1[:, :, 0:TPB])

            def modulation_rows():
                dve.wait_ge(p_mod, 1)
                for n in range(1, 3):
                    link(V.tensor_copy(mod_sb[:, n * 512:(n + 1) * 512], bank[4 + n][0:B, :]))
                link(V.tensor_scalar(mod_sb[:, 4 * H:5 * H], mod_sb[:, 4 * H:5 * H], 1.0, None, ALU.add))
                for n in (2, 5):
                    g = mod_sb[:, n * H:(n + 1) * H]
                    link(V.tensor_scalar(mod_t[:, 0, :], g, 0.0, 2.0, ALU.is_ge, ALU.mult))
                    link(V.tensor_scalar(mod_t[:, 0, :], mod_t[:, 0, :], 1.0, None, ALU.subtract))
                    link(V.scalar_tensor_tensor(mod_t[:, 1, :], g, -1.0, g, ALU.mult, ALU.max))
                    ins = V.scalar_tensor_tensor(g, mod_t[:, 1, :], 0.25, mod_t[:, 0, :], ALU.max, ALU.mult)
                    if n == 2:
                        link(ins)
                    else:
                        ins.then_inc(v_mod, 1)

            def normalise(it):
                for t in range(TPB):
                    n = TPB * it + t
                    ins = V.tensor_scalar(xn[:, t, :], x_sb[:, n, :], mv1[:, n, 0:1], rs1[:, 3, bass.ts(n, 1)],
                                          ALU.subtract, ALU.mult)
                    if t == TPB - 1:
                        ins.then_inc(v_xn, 1)
                    else:
                        link(ins)

            def rope_tile(it, t):
                dve.wait_ge(p_qkv, TPB * it + t + 1)
                qk = bank[1 + t][:, :]
                pairs = qk.rearrange("p (m i two) -> p m i two", i=D // 2, two=2)
                r2 = rope2.rearrange("p (m i two) -> p m i two", i=D // 2, two=2)
                heads = 2 * NH
                cos = rope_sb[:, t, 0, None, :].broadcast_to([P, heads, D])
                sin = rope_sb[:, t, 1, :].rearrange("p (i two) -> p i two", two=2)
                link(V.tensor_tensor(rope1[:, t, :].rearrange("p (m d) -> p m d", d=D),
                                     qk.rearrange("p (m d) -> p m d", d=D), cos, ALU.mult))
                for o in range(2):
                    link(V.tensor_tensor(r2[:, :, :, o], pairs[:, :, :, 1 - o],
                                         sin[:, None, :, o].broadcast_to([P, heads, D // 2]), ALU.mult))
                V.tensor_tensor(rope1[:, t, :], rope1[:, t, :], rope2, ALU.add).then_inc(v_rope, 1)
                dve.wait_ge(v_rope, TPB * it + t + 1)

            def low(it, t):
                dve.wait_ge(a_hi, 2 * (TPB * it + t + 1))
                link(V.tensor_tensor(q_split[:, t, :, 2:4, :], rope_part(t, 0), q_split[:, t, :, 0:2, :], ALU.subtract))
                V.tensor_tensor(k_split[:, t, :, 1::2, :], rope_part(t, 1), k_split[:, t, :, 0::2, :],
                                ALU.subtract).then_inc(v_split, 1)

            def q_copy(it, t):
                dve.wait_ge(p_qkT, 4 * it + 2 * t + 1)
                src = bank16[(1, 2)[t]].rearrange("p (g q) -> p g q", q=P)
                V.tensor_copy(qT[:, :, t * P:(t + 1) * P], src).then_inc(v_qT, 1)

            def maxima(it, n0, n1):
                for n in range(n0, n1):
                    par, half = n // 6, n // 3 % 2
                    i0, nh, qt = ((0, 4, 0), (0, 2, 1), (2, 2, 1))[n % 3]
                    dve.wait_ge(p_s1, 12 * it + n + 1)
                    w = (qt + 1) * P
                    src = bank[4 + n % 3][:, 0:nh * w].rearrange("p (h k) -> p h k", k=w)
                    h0 = par + 8 * half + 2 * i0
                    V.tensor_reduce(rmax[:, qt, h0:h0 + 2 * nh - 1:2], src, AX.X, ALU.max).then_inc(v_max, 1)

            def split_maxima(it):
                dve.wait_ge(v_max, 12 * (it + 1))
                link(V.tensor_scalar(negr[:, 0, :, :], rmax[:, :, :], -1.0, None, ALU.mult))
                for part in range(3):
                    src = negr[:, part % 2, :, :]
                    link(V.tensor_copy(neg3[:, :, 0, part, :], src))
                    if part < 2:
                        link(V.tensor_tensor(negr[:, 1 - part % 2, :, :], src, neg3[:, :, 0, part, :], ALU.subtract))
                V.tensor_copy(neg3[:, :, 1, 0:3, :], neg3[:, :, 0, 0:3, :]).then_inc(v_neg, 1)

            def attention_out(b):
                for t in range(TPB):
                    dve.wait_ge(p_attq, TPB * b + t + 1)
                    src = bank[4 + t][:, :].rearrange("p (m c) -> p m c", c=32)
                    link(V.reciprocal(rden[:, t, :], src[:, :, D]))
                    dst = att_tok[:, t, :].rearrange("p (m par d) -> p par m d", par=2, d=D)
                    V.tensor_tensor(dst, src[:, :, 0:D].rearrange("p (par m) d -> p par m d", par=2),
                                    rden[:, t, :].rearrange("p (par m o) -> p par m o", par=2, o=1).broadcast_to([P, 2, NH // 2, D]),
                                    ALU.mult).then_inc(v_att, 1)

            def residual(b):
                dve.wait_ge(p_o, b + 1)
                dve.wait_ge(s_mb, 32)
                xb = x_sb[:, bass.ts(b, TPB), :]
                link(V.tensor_tensor(r2, bank[7][:, :].rearrange("p (t h) -> p t h", t=TPB), mrow(b, 0), ALU.mult))
                link(V.tensor_tensor(xb, xb, r2, ALU.add))
                for t in range(TPB):
                    link(V.bn_stats(stats[:, t, :], x_sb[:, TPB * b + t, :]))
                for t in range(TPB):
                    link(V.bn_aggr(mv2[:, t, :], stats[:, t, :]))
                V.tensor_scalar(rs2[:, 0, :], mv2[:, :, 1], EPS, None, ALU.add).then_inc(v_x2, 1)

            def hidden_rows(b):
                dve.wait_ge(g_free, b + 1)
                dve.wait_ge(a_rs2, b + 1)
                refine(rs2)
                for t in range(TPB):
                    link(V.tensor_scalar(r2[:, t, :], x_sb[:, TPB * b + t, :], mv2[:, t, 0:1], rs2[:, 3, t:t + 1],
                                         ALU.subtract, ALU.mult))
                link(V.tensor_tensor(r2, r2, mrow(b, 2), ALU.mult))
                V.tensor_tensor(rows[:, :, 0:H], r2, mrow(b, 1), ALU.add).then_inc(v_h2, 1)

            def picks(b):
                dve.wait_ge(p_log, b + 1)
                link(V.tensor_copy(logit[:, :, :], bank[7][:, 0:TPB * E].rearrange("p (t e) -> p t e", t=TPB)))
                for t in range(TPB):
                    link(V.max(top8[:, t, :], logit[:, t, :]))
                V.tensor_scalar(rows[:, :, H:H + 1], top8[:, :, 0:1], -1.0, None, ALU.mult).then_inc(v_top, 1)
                for t in range(TPB):
                    link(V.match_replace(logit_rep[:, t, :], top8[:, t, :], logit[:, t, :], FAR))
                link(V.tensor_tensor(sel[:, :, :], logit[:, :, :], logit_rep[:, :, :], ALU.not_equal))
                for t in range(TPB - 1):
                    link(V.tensor_tensor(seen[:, t + 1, :], seen[:, t, :], sel[:, t, :], ALU.add))
                dve.wait_ge(vch, n_chain())
                V.tensor_copy(code[:, 0, :, :], sel[:, :, :]).then_inc(v_sel, 1)

            def slots(b):
                dve.wait_ge(p_cum, b + 1)
                rank = bank[7][:, 256:256 + TPB * E].rearrange("p (t e) -> p t e", t=TPB)
                link(V.scalar_tensor_tensor(code[:, 0, :, :], rank, float(CAP), sel[:, :, :], ALU.is_le, ALU.mult))
                base = cst[:, None, 4 * P + NH:4 * P + NH + E].broadcast_to([P, TPB, E])
                V.scalar_tensor_tensor(code[:, 1, :, :], rank, -1.0, base, ALU.mult, ALU.add).then_inc(v_rank, 1)
                dve.wait_ge(v_rank, b + 2)
                link(V.tensor_tensor(code[:, 0, :, :], code[:, 0, :, :], code[:, 1, :, :], ALU.mult))
                link(V.tensor_tensor(seen[:, 0, :], seen[:, TPB - 1, :], sel[:, TPB - 1, :], ALU.add))
                for t in range(TPB):
                    link(V.max(code8[:, t, :], code[:, 0, t, :]))
                dve.wait_ge(a_sum, TPB * (b + 1))
                link(V.reciprocal(rows[:, :, H + 1], sum8[:, :]))
                link(V.tensor_copy(rows[:, :, H + 2:H + 3].bitcast(I32),
                                   tok[:, bass.ts(b, TPB)].rearrange("p (t o) -> p t o", o=1)))
                for t in range(TPB):
                    V.tensor_scalar(slot_idx[:, t, :], code8[:, t, :], -1.0, float(BIGSLOT), ALU.mult, ALU.add).then_inc(v_slot, 1)

            def n_chain():
                return chain_count[0]

            chain_count = [0]
            plain_link, plain_clear = link, clear

            def link(ins):
                chain_count[0] += 1
                plain_link(ins)

            def clear():
                chain_count[0] = 0
                plain_clear()

            r2 = rope2.rearrange("p (t h) -> p t h", t=TPB)

            def mrow(b, n):
                return modB[:, bass.ts(b, 1), n * H:(n + 1) * H].broadcast_to([P, TPB, H])

            normalise(0)
            V.memset(seen[:, :, :], 0.0).then_inc(v_rank, 1)
            dve.wait_ge(v_rank, 1)
            link(V.memset(neg3[:, :, :, :, :], 0.0))
            V.tensor_copy(pickb[:, :, :], cst[:, 4 * P:4 * P + NH, None].broadcast_to([P, NH, P])).then_inc(v_csts, 1)
            dve.wait_ge(s_x, 16)
            statistics(TPB, B * TPB)
            rope_tile(0, 0)
            rope_tile(0, 1)
            low(0, 0)
            low(0, 1)
            dve.wait_ge(a_rs1, 2)
            refine(rs1[:, :, TPB:])
            q_copy(0, 0)
            q_copy(0, 1)
            modulation_rows()
            normalise(1)
            maxima(0, 0, 12)
            split_maxima(0)

            def one_round(it, more):
                b = it - 1
                rope_tile(it, 0)
                rope_tile(it, 1)
                low(it, 0)
                low(it, 1)
                q_copy(it, 0)
                attention_out(b)
                q_copy(it, 1)
                if more:
                    normalise(it + 1)
                residual(b)
                maxima(it, 0, 3)
                hidden_rows(b)
                maxima(it, 3, 8)
                picks(b)
                maxima(it, 8, 12)
                split_maxima(it)
                slots(b)

            with dve.Fori(1, B - 1) as it:
                clear()
                one_round(it, True)
            clear()
            one_round(B - 1, False)
            clear()
            attention_out(B - 1)
            residual(B - 1)
            hidden_rows(B - 1)
            picks(B - 1)
            slots(B - 1)

            def expert_steps(i, j, first, last_):
                s = GRP * i + j
                if not (first and j < 1) and not (last_ and j > 0):
                    q = (j - 1) % GRP
                    gu = bank[2 + q % 2]
                    dve.wait_ge(a_w, s)
                    if not (first and j < 3):
                        dve.wait_ge(p_hidT, s - 2)
                    link(V.scalar_tensor_tensor(hid0[:, q % 2, :], tanhg[:, q % 2, :], 1.0, gu[:, 0:I], ALU.add, ALU.mult))
                    V.scalar_tensor_tensor(hid[:, q % 2, :], hid0[:, q % 2, :], 0.5, gu[:, I:GU],
                                           ALU.mult, ALU.mult).then_inc(v_hid, 1)
                if not (first and j < 3):
                    q = (j - 3) % GRP
                    dve.wait_ge(p_ye, s - 2)
                    dve.wait_ge(a_w, s - 2)
                    if not (first and j < 3 + NACC):
                        dve.wait_ge(added[q % NACC], 16 * (2 * i + (-1 if j < 3 else (j - 3) // NACC)))
                    V.tensor_scalar(ye[:, q % NACC, :], bank[6 + q % 2][:, 0:H], gatew[:, q:q + 1], xe[:, q, H + 1:H + 2],
                                    ALU.mult, ALU.mult).then_inc(v_ye, 1)

            clear()
            for j in range(GRP):
                expert_steps(0, j, True, False)
            with dve.Fori(1, E // GRP) as i:
                clear()
                for j in range(GRP):
                    expert_steps(i, j, False, False)
            clear()
            for j in range(3):
                expert_steps(E // GRP, j, False, True)

            dve.wait_ge(sum_ld, 16 * NACC)
            part = [arena[:, a * TOK * 2:(a + 1) * TOK * 2].rearrange("p (n h) -> p n h", h=H) for a in range(NACC)]
            for b in range(B):
                ts = slice(TPB * b, TPB * b + TPB)
                link(V.tensor_tensor(part[0][:, ts, :], part[0][:, ts, :], part[1][:, ts, :], ALU.add))
                link(V.tensor_tensor(part[2][:, ts, :], part[2][:, ts, :], part[3][:, ts, :], ALU.add))
                link(V.tensor_tensor(part[0][:, ts, :], part[0][:, ts, :], part[2][:, ts, :], ALU.add))
                link(V.tensor_tensor(part[0][:, ts, :], part[0][:, ts, :],
                                     gbB[:, bass.ts(b, 1), :].broadcast_to([P, TPB, H]), ALU.mult))
                V.tensor_tensor(x_sb[:, ts, :], x_sb[:, ts, :], part[0][:, ts, :], ALU.add).then_inc(v_out, 1)


def kernel(**inputs):
    import numpy as np
    import concourse.bacc as bacc
    from concourse.bass_utils import run_bass_kernel_spmd

    a = {n.removeprefix("L0_"): np.asarray(v) for n, v in inputs.items()}
    f32 = np.float32
    B, S, H = a["attn_x"].shape
    D, P, E, CAP = 16, 128, a["ffn_router_weight"].shape[0], 128
    half = D // 2
    inv = (1.0 / np.float32(10000.0) ** (np.arange(half, dtype=f32) / f32(half))).astype(f32)
    ang = np.arange(S, dtype=f32)[:, None] * inv[None, :]
    cos = np.repeat(np.cos(ang), 2, axis=-1)
    sin = np.repeat(np.sin(ang), 2, axis=-1)
    sin[:, 0::2] *= -1
    rope = np.stack([cos, sin], 1).astype(f32)
    r = np.arange(P)
    consts = np.concatenate([
        np.eye(P),
        np.where(r[None, :] <= r[:, None], 0.0, -1e30),
        np.where(r[None, :] >= r[:, None], 0.0, -1e30),
        r[:, None] <= r[None, :],
        (r[:, None] % 64 % 16 == np.arange(16)[None, :]) & (r[:, None] % 64 < 48),
        np.broadcast_to(2 * E * CAP + 1 - CAP * np.arange(E), (P, E)),
    ], 1).astype(f32)
    token_ids = (r[:, None] + P * np.arange(B * S // P + 1)[None, :]).astype(np.int32)
    arrays = {
        "x": a["attn_x"],
        "wqkvT": np.ascontiguousarray(np.concatenate([a["attn_Wq"], a["attn_Wk"], a["attn_Wv"]], 0).T),
        "bias": np.concatenate([a["attn_bq"], a["attn_bk"], a["attn_bv"], a["attn_bo"]])[None, :],
        "woT": np.ascontiguousarray(a["attn_Wo"].T),
        "routerT": np.ascontiguousarray(a["ffn_router_weight"].T),
        "gate_up": a["ffn_gate_up_proj"],
        "down": a["ffn_down_proj"],
        "cond": np.ascontiguousarray(a["c"].T.reshape(H // P, P, B).transpose(1, 0, 2)),
        "wmod": a["wmod"],
        "rope": rope,
        "consts": consts,
        "token_ids": token_ids,
    }
    nc = bacc.Bacc("TRN2", target_bir_lowering=False, num_devices=1)
    args = [nc.dram_tensor(f"in_{n}", v.shape, mybir.dt.from_np(v.dtype), kind="ExternalInput").ap()
            for n, v in arrays.items()]
    args.append(nc.dram_tensor("out_y", (B, S, H), mybir.dt.float32, kind="ExternalOutput").ap())
    adaln_moe_program(nc, *args)
    got = run_bass_kernel_spmd(nc, [{f"in_{n}": v for n, v in arrays.items()}], core_ids=[0])
    return got.results[0]["out_y"]
```

```python
import concourse.bass as bass
from concourse import mybir
from contextlib import ExitStack


def adaln_moe_program(nc, x, wqkvT, bias, woT, routerT, gate_up, down, cond, wmod,
                      rope, consts, token_ids, out):
    FP32, BF16, FP16 = mybir.dt.float32, mybir.dt.bfloat16, mybir.dt.float16
    I32, U32 = mybir.dt.int32, mybir.dt.uint32
    ACT, ALU, AX = mybir.ActivationFunctionType, mybir.AluOpType, mybir.AxisListType

    B, S, H = x.shape
    P = 128
    TPB = S // P
    HC = H // P
    NH = 16
    D = H // NH
    E, _, GU = gate_up.shape
    I = GU // 2
    K = 8
    CAP = 128
    TOK = B * S
    SLOTS = E * CAP
    ROW = H + 4
    NACC = 4
    ACCROWS = TOK + CAP
    EW = HC * (GU + 1) + H
    EARLY = 32
    GRP = 8
    SCALE = 1.0 / float(D) ** 0.5
    EPS = 1e-5
    FAR = -3.0e38
    BIGSLOT = 2 * SLOTS

    slot_rows = nc.dram_tensor("slot_rows", [SLOTS, ROW], FP32, kind="Internal").ap()
    sums = [nc.dram_tensor(f"sum{a}", [ACCROWS, H], FP32, kind="Internal").ap() for a in range(NACC)]
    BY_POOL = 1
    LAST = GRP
    mod_dram = nc.dram_tensor("mod_rows", [B, 6 * H], FP32, kind="Internal").ap()

    ctx = ExitStack()
    with ctx:
        def sb(name, shape, dt=FP32):
            return ctx.enter_context(nc.sbuf_tensor(name, shape, dt))

        def sem(name):
            return ctx.enter_context(nc.semaphore(name))

        arena = sb("arena", [P, E * EW])
        x_sb = sb("x_sb", [P, B * TPB, H])
        gbB = sb("gbB", [P, B, H])
        rows = sb("rows", [P, TPB, ROW])
        cst = sb("cst", [P, 4 * P + NH + E])
        ident = cst[:, 0:P]
        tok = sb("tok", [P, B * TPB + 1], I32)
        router_sb = sb("router_sb", [P, HC, E])
        zero_row = sb("zero_row", [P, ROW])

        expert_w = arena[:, :].rearrange("p (e w) -> p e w", w=EW)

        NXE = 8
        stage = sb("stage", [P, NXE * (ROW + 5) + 2 * HC * CAP + 6 * I + 2 * CAP + NACC * H])

        def region(whole, at, limit):
            cur = [at]

            def take(shape, dt=FP32, parts=P):
                n = 1
                for d in shape:
                    n *= d
                w = n * (2 if dt in (BF16, FP16) else 4) // 4
                v = whole[0:parts, cur[0]:cur[0] + w]
                cur[0] += w
                assert cur[0] <= limit
                v = v if dt == FP32 else v.bitcast(dt)
                names = "abcde"[:len(shape)]
                if len(shape) == 1:
                    return v
                return v.rearrange("p (" + " ".join(names) + ") -> p " + " ".join(names), **dict(zip(names, shape)))
            return take

        ffn = region(stage, 0, stage.shape[1])
        xe = ffn([NXE, ROW])
        xeT = ffn([2, HC * CAP])
        tanhg = ffn([2, I])
        hid0 = ffn([2, I])
        hid = ffn([2, I])
        hidT = ffn([2, CAP], parts=I)
        gatew = ffn([NXE])
        meta = ffn([NXE, 4])
        ye = ffn([NACC, H])

        SC = TPB * S - P
        scratch = region(arena, EARLY * EW, E * EW)
        probT = scratch([2, 4 * SC])
        v_aug = scratch([TPB, NH, 32])
        qT = scratch([NH // 2, S], FP16)
        kT = scratch([NH // 2, S], FP16)
        h1T = scratch([HC, S])
        xn = scratch([TPB, H])
        rope1 = scratch([TPB, 2 * H])
        rope2 = scratch([2 * H])
        q_split = scratch([TPB, NH, 4, D], FP16)
        k_split = scratch([TPB, NH, 4, D], FP16)
        att_sb = scratch([2, 512])
        att_tok = scratch([TPB, H])
        attT = scratch([HC, S])
        wqkv_sb = scratch([HC, 3 * H])
        wo_sb = scratch([HC, H])
        modB = scratch([B, 3 * H])
        h2T = scratch([HC, S])
        mod_sb = scratch([6 * H], parts=B)
        before = region(arena, EARLY * EW, EARLY * EW + 2 * 4 * SC)
        wmod_sb = before([HC, 6 * H])
        at = EARLY * EW + 2 * 4 * SC + TPB * NH * 32
        before = region(arena, at, at + NH * S)
        bias_p = before([3, P], BF16, parts=4 * H // P)
        at += NH * S // 2 + HC * S + TPB * H + (TPB + 1) * 2 * H + TPB * NH * 4 * D
        before = region(arena, at, at + 8 * H)
        bias_f = before([2, P], parts=4 * H // P)

        at += 2 * 512
        before = region(arena, at, at + 4 * H)
        mod_t = before([2, 2, H], parts=B)

        early = region(stage, 0, stage.shape[1])
        rope_sb = sb("rope_sb", [P, TPB, 2, D])
        sent = early([TPB, ROW])
        sent_idx = early([TPB, K], U32)
        ident16 = early([P], FP16)
        identb = early([P], BF16)
        maskb = early([P], BF16)
        maskTb = early([P], BF16)
        prefixb = early([P], BF16)
        onesb = sb("onesb", [P, P], BF16)[:, :]
        pickb = early([NH, P], BF16)
        ones3 = early([P], BF16, parts=3)
        bias3 = early([4 * H], BF16, parts=3)
        condT = sb("condT", [P, 4, HC, B])
        modT = sb("modT", [P, 4, B])
        stats = sb("stats", [P, B * TPB, 6])
        mv1 = sb("mv1", [P, B * TPB, 2])
        rs1 = sb("rs1", [P, 4, B * TPB])
        mv2 = sb("mv2", [P, TPB, 2])
        rs2 = sb("rs2", [P, 4, TPB])
        rmax = sb("rmax", [P, TPB, NH])
        negr = early([TPB, NH])
        neg2 = early([TPB, 2, 4, NH], BF16)
        negT = early([S], BF16)
        rden = sb("rden", [P, TPB, NH])
        logit = early([TPB, E])
        logit_rep = early([TPB, E])
        top8 = sb("top8", [P, TPB, K])
        exp8 = sb("exp8", [P, TPB, K])
        sum8 = sb("sum8", [P, TPB])
        sel = early([TPB, E], BF16)
        seen = early([TPB + 1, E], BF16)
        code = early([2, TPB, E])
        code8 = sb("code8", [P, TPB, K])
        slot_idx = sb("slot_idx", [P, TPB, K], U32)

        bank = [ctx.enter_context(nc.psum_tensor(f"bank{i}", [P, 512], FP32)) for i in range(8)]
        bank16 = [b[:, :].bitcast(FP16) for b in bank]
        bankb = [b[:, :].bitcast(BF16) for b in bank]

        s_c = sem("consts_loaded")
        s_m = sem("wmod_loaded")
        s_x0 = sem("first_x_loaded")
        s_x = sem("x_loaded")
        s_w2 = sem("wo_and_router_loaded")
        s_w = sem("attn_weights_loaded")
        s_bias = sem("bias_loaded")
        s_b3 = sem("bias3_moved")
        s_md = sem("mod_stored")
        s_mb = sem("mod_broadcast")
        s_ew = sem("early_experts_loaded")
        s_lw = [sem(f"late_experts_loaded{n}") for n in range(3)]
        s_fill = sem("slots_filled")
        s_zero = sem("zero_row_ready")
        vch = sem("vector_chain")
        ach = sem("scalar_chain")
        gch = sem("gpsimd_chain")
        g_csts = sem("consts_converted")
        g_zv = sem("v_zeroed")
        s_ct = sem("cond_loaded")
        s_m0 = sem("wmod_front_loaded")
        a_tanh = sem("tanh_cond")
        v_silu = sem("silu_ready")
        p_mod = sem("mod_in_banks")
        a_mod = sem("mod_rows_copied")
        v_mod = sem("mod_ready")
        p_modT = sem("modT_in_bank")
        v_modT = sem("modT_ready")
        g_bias = sem("bias_split")
        v_var1 = sem("variance1_ready")
        a_rs1 = sem("rstd1_guess")
        v_xn = sem("xn_ready")
        p_xnT = sem("xnT_in_bank")
        a_h1T = sem("h1T_ready")
        p_qkv = sem("qkv_in_banks")
        v_rope = sem("rope_ready")
        a_hi = sem("high_parts_ready")
        v_split = sem("split_ready")
        a_vaug = sem("v_ready")
        p_qkT = sem("qkT_in_banks")
        v_qT = sem("qT_ready")
        a_kT = sem("kT_ready")
        p_s1 = sem("scores_for_max")
        v_max = sem("max_taken")
        v_neg = sem("neg_max_split")
        p_negT = sem("neg_max_T")
        a_negT = sem("neg_max_T_ready")
        p_s2 = sem("scoresT_in_bank")
        a_exp = sem("probs_ready")
        p_pv = sem("pv_done")
        a_att = sem("att_copied")
        p_attq = sem("att_token_major")
        v_att = sem("att_normalised")
        p_attT = sem("attT_in_bank")
        a_attT = sem("attT_ready")
        p_o = sem("o_proj_done")
        v_x2 = sem("x2_variance")
        a_rs2 = sem("rstd2_guess")
        v_h2 = sem("h2_ready")
        p_h2T = sem("h2T_in_bank")
        a_h2T = sem("h2T_ready")
        p_log = sem("logits_in_bank")
        v_top = sem("top8_ready")
        a_sum = sem("sum8_ready")
        v_sel = sem("picks_ready")
        p_cum = sem("ranks_in_bank")
        v_ones = sem("ones_ready")
        v_rank = sem("ranks_bank_free")
        v_slot = sem("slots_ready")
        g_sent = sem("rows_moved")
        g_free = sem("rows_free")
        g_scat = sem("rows_scattered")
        g_rcol = sem("router_columns")
        xe_ld = [sem(f"slot_rows_loaded{j}") for j in range(NXE)]
        v_meta = sem("meta_copied")
        p_xeT = sem("xeT_in_bank")
        a_xeT = sem("xeT_ready")
        p_gu = sem("gate_up_in_bank")
        a_tg = sem("tanh_gate_ready")
        a_w = sem("gate_weight_ready")
        v_hid = sem("hidden_ready")
        p_hidT = sem("hiddenT_in_bank")
        a_hidT = sem("hiddenT_ready")
        p_ye = sem("expert_out_in_bank")
        v_ye = sem("expert_out_ready")
        added = [sem(f"added{a}") for a in range(NACC)]
        sum_ld = [[sem(f"sums_loaded{n}_{b}") for b in range(B)] for n in range(2)]
        v_pair = sem("first_pair_added")
        g_out = sem("gpsimd_out_ready")
        v_out = sem("out_ready")
        s_out = sem("out_stored")

        groups = [[par + 8 * half + 2 * i for i in range(4)] for par in range(2) for half in range(2)]
        row0 = [64 * (g // 2) for g in range(4)]

        part = arena[:, 0:NACC * B * TPB * H].rearrange("p (n b a t h) -> p n b a t h", n=2, b=B, a=2, t=TPB)

        def sum_of(e):
            return e % NACC if e < E - LAST else e % 2

        def adds_before(e, a):
            return sum(1 for n in range(e) if sum_of(n) == a)

        ALL = range(TPB)
        chunks = [(g, 0, 4, 0) for g in range(4)] + [(g, i0, 2, 1) for g in range(4) for i0 in (0, 2)]

        def back_bank(what, alt):
            return bank[{"attT": (6, 3), "o": (7, 1), "h2T": (0, 2), "router": (7, 1)}[what][alt]]

        def tiles(ts):
            return slice(ts[0], ts[-1] + 1)

        def rope_part(t, n):
            return (rope1[:, t, n * H:(n + 1) * H].rearrange("p (h o d) -> p h o d", h=NH, o=1)
                    .broadcast_to([P, NH, 2, D]))

        block = ctx.enter_context(nc.Block())

        def linker(eng, chain):
            n = [0]

            def link(ins):
                n[0] += 1
                ins.then_inc(chain, 1)
                eng.wait_ge(chain, n[0])

            def clear():
                eng.sem_clear(chain)
                n[0] = 0
            return link, clear

        @block.sync
        def _(sp):
            wm = wmod.rearrange("(k p) n -> p k n", p=P)
            xr = x.rearrange("b (t p) h -> p (b t) h", p=P)
            sp.dma_start(condT[:, 0, :, :], cond).then_inc(s_ct, 16)
            sp.dma_start(bias_f[:, 0, :], bias).then_inc(s_bias, 16)
            sp.dma_start(x_sb[:, 0:TPB, :], xr[:, 0:TPB, :]).then_inc(s_x0, 16)
            sp.dma_start(wmod_sb[:, :, 0:2 * H], wm[:, :, 0:2 * H]).then_inc(s_m0, 16)
            sp.dma_start(cst[:, :], consts).then_inc(s_c, 16)
            sp.dma_start(tok[:, :], token_ids).then_inc(s_c, 16)
            sp.dma_start(rope_sb[:, :, :, :], rope.rearrange("(t p) a d -> p t a d", p=P)).then_inc(s_c, 16)
            sp.wait_ge(g_bias, 1)
            for third in range(3):
                sp.dma_start(bias3[third:third + 1, :].rearrange("c (k n) -> c k n", n=P),
                             bias_p[:, third, :]).then_inc(s_b3, 16)
            sp.dma_start(wqkv_sb, wqkvT.rearrange("(k p) n -> p k n", p=P)).then_inc(s_w, 16)
            sp.dma_start(x_sb[:, TPB:, :], xr[:, TPB:, :]).then_inc(s_x, 16)
            sp.dma_start(wmod_sb[:, :, 2 * H:], wm[:, :, 2 * H:]).then_inc(s_m, 16)
            sp.dma_start(wo_sb, woT.rearrange("(k p) n -> p k n", p=P)).then_inc(s_w2, 16)
            sp.dma_start(router_sb[:, :, :], routerT.rearrange("(k p) n -> p k n", p=P)).then_inc(s_w2, 16)
            def load_experts(e0, n, s):
                some = bass.ds(e0, n)
                for k in range(HC):
                    sp.dma_start(expert_w[:, some, k * (GU + 1):k * (GU + 1) + GU],
                                 gate_up[some, k * P:(k + 1) * P, :].rearrange("e p f -> p e f")).then_inc(s, 16)
                sp.dma_start(expert_w[0:I, some, HC * (GU + 1):EW],
                             down[some, :, :].rearrange("e i h -> i e h")).then_inc(s, 16)

            sp.wait_ge(s_zero, 1)

            def fill_slots(n):
                sp.dma_start(slot_rows[n * 1024:(n + 1) * 1024, :].rearrange("(e c) r -> c e r", c=CAP),
                             zero_row[:, None, :].broadcast_to([P, 8, ROW])).then_inc(s_fill, 16)

            for n in range(2):
                fill_slots(n)
            sp.wait_ge(v_mod, 1)
            sp.dma_start(mod_dram[:, 2 * H:], mod_sb[:, 2 * H:]).then_inc(s_md, 16)
            sp.wait_ge(s_md, 16)
            sp.dma_start(modB, mod_dram[None, :, 2 * H:5 * H].broadcast_to([P, B, 3 * H])).then_inc(s_mb, 16)
            sp.dma_start(gbB[:, :, :], mod_dram[None, :, 5 * H:6 * H].broadcast_to([P, B, H])).then_inc(s_mb, 16)
            for n in range(2, 8):
                fill_slots(n)
            for a in range(NACC):
                sp.dma_start(sums[a].rearrange("(n p) h -> p n h", p=P),
                             zero_row[:, None, 0:H].broadcast_to([P, ACCROWS // P, H])).then_inc(s_fill, 16)
            for e0 in range(0, EARLY, GRP):
                load_experts(e0, GRP, s_ew)
            sp.wait_ge(v_slot, B * TPB)
            load_experts(EARLY, GRP, s_lw[0])
            sp.wait_ge(g_scat, 16 * K * B * TPB)

            def load_slots(i, j, first):
                e = GRP * i + j
                if not first:
                    sp.wait_ge(v_meta, e - GRP + 1)
                    sp.wait_ge(p_xeT, e - GRP + 1)
                sp.dma_start(xe[:, j, :], slot_rows.rearrange("(e c) r -> c e r", c=CAP)[:, e, :]).then_inc(xe_ld[j], 16)

            for j in range(GRP):
                load_slots(0, j, True)

            def load_eight(i, s, first_expert, every):
                for j in range(GRP):
                    load_slots(i, j, False)
                    if s is not None and j % every == 0:
                        load_experts(first_expert + 2 * j // every, 2, s)

            load_eight(1, s_lw[1], EARLY + GRP, 2)
            with sp.Fori(2, 6) as i:
                load_eight(i, s_lw[2], EARLY + GRP + 4 * i, 4)
            with sp.Fori(6, E // GRP) as i:
                load_eight(i, None, None, None)
            for pair in (1, 0):
                for a in (2 * pair, 2 * pair + 1):
                    sp.wait_ge(added[a], 16 * adds_before(E, a))
                for b in range(B):
                    for a in range(2):
                        sp.dma_start(part[:, pair, b, a, :, :],
                                     sums[2 * pair + a][b * S:(b + 1) * S, :].rearrange("(t p) h -> p t h", p=P)
                                     ).then_inc(sum_ld[pair][b], 16)
            for b in (0, 2, BY_POOL, 3):
                if b == BY_POOL:
                    sp.wait_ge(g_out, 1)
                else:
                    sp.wait_ge(v_out, (1, None, 2, 3)[b])
                sp.dma_start(out[b].rearrange("(t p) h -> p t h", p=P), x_sb[:, bass.ts(b, TPB), :]).then_inc(s_out, 16)
            sp.wait_ge(s_out, 16 * B)

        @block.gpsimd
        def _(pool):
            link, clear = linker(pool, gch)
            nc.gpsimd.memset(ones3, 1.0)
            pool.wait_ge(s_bias, 16)
            link(nc.gpsimd.tensor_copy(bias_p[:, 0, :], bias_f[:, 0, :]))
            link(nc.gpsimd.tensor_tensor(bias_f[:, 1, :], bias_f[:, 0, :], bias_p[:, 0, :], ALU.subtract))
            link(nc.gpsimd.tensor_copy(bias_p[:, 1, :], bias_f[:, 1, :]))
            link(nc.gpsimd.tensor_tensor(bias_f[:, 0, :], bias_f[:, 1, :], bias_p[:, 1, :], ALU.subtract))
            nc.gpsimd.tensor_copy(bias_p[:, 2, :], bias_f[:, 0, :]).then_inc(g_bias, 1)
            link(nc.gpsimd.memset(zero_row[:, :], 0.0))
            pool.wait_ge(s_c, 48)
            nc.gpsimd.tensor_copy(zero_row[:, H + 2:H + 3].bitcast(I32), tok[:, B * TPB:B * TPB + 1]).then_inc(s_zero, 1)

            def fresh_rows(b):
                nc.gpsimd.memset(rows[:, :, H + 3:H + 4], 0.0)
                nc.gpsimd.tensor_copy(rows[:, :, H + 2:H + 3].bitcast(I32),
                                      tok[:, TPB * b:TPB * (b + 1)].rearrange("p (t o) -> p t o", o=1)).then_inc(g_free, 1)

            fresh_rows(0)
            nc.gpsimd.tensor_copy(ident16, ident)
            nc.gpsimd.memset(v_aug, 0.0).then_inc(g_zv, 1)
            pool.wait_ge(g_zv, 1)
            nc.gpsimd.memset(v_aug[:, :, :, D:D + 1], 1.0)
            nc.gpsimd.tensor_copy(identb, ident)
            nc.gpsimd.tensor_copy(maskb, cst[:, P:2 * P]).then_inc(g_csts, 1)
            nc.gpsimd.tensor_copy(maskTb, cst[:, 2 * P:3 * P])
            nc.gpsimd.tensor_copy(prefixb, cst[:, 3 * P:4 * P])
            nc.gpsimd.tensor_copy(pickb[:, :, :], cst[:, 4 * P:4 * P + NH, None].broadcast_to([P, NH, P])).then_inc(g_csts, 1)
            pool.wait_ge(s_w2, 32)

            def router_columns(e0, e1):
                for k in range(HC):
                    c = k * (GU + 1) + GU
                    nc.gpsimd.tensor_copy(expert_w[:, e0:e1, c:c + 1],
                                          router_sb[:, k, e0:e1].rearrange("p (e o) -> p e o", o=1)).then_inc(g_rcol, 1)

            router_columns(0, EARLY)
            pool.wait_ge(s_fill, 16 * (8 + NACC))

            def scatter(b):
                src, idx = rows, slot_idx
                pool.wait_ge(g_free, b + 1)
                if b < B - 1:
                    pool.wait_ge(v_slot, TPB * (b + 1))
                    nc.gpsimd.tensor_copy(sent_idx[:, :, :], slot_idx[:, :, :])
                    nc.gpsimd.tensor_copy(sent[:, :, :], rows[:, :, :]).then_inc(g_sent, 1)
                    pool.wait_ge(g_sent, b + 1)
                    fresh_rows(b + 1)
                    src, idx = sent, sent_idx
                for t in range(TPB):
                    pool.wait_ge(v_slot, TPB * b + t + 1)
                    for k in range(K):
                        pool.indirect_dma_start(
                            slot_rows, bass.IndirectOffsetOnAxis(ap=idx[:, t, k:k + 1], axis=0),
                            src[:, t, :], None, bounds_check=SLOTS - 1, oob_is_err=False).then_inc(g_scat, 16)

            for b in range(B):
                scatter(b)
                pool.wait_ge(g_scat, 16 * K * (b + 1) * TPB)
            router_columns(EARLY, E)

            def add_expert(e):
                a, j = sum_of(e), e % GRP
                pool.wait_ge(v_ye, e + 1)
                if adds_before(e, a):
                    pool.wait_ge(added[a], 16 * adds_before(e, a))
                pool.indirect_dma_start(
                    sums[a], bass.IndirectOffsetOnAxis(ap=meta[:, j, 2:3].bitcast(U32), axis=0),
                    ye[:, j % NACC, :], None, bounds_check=ACCROWS - 1, oob_is_err=True,
                    compute_op=ALU.add).then_inc(added[a], 16)

            for e in range(E):
                add_expert(e)
            ts = slice(TPB * BY_POOL, TPB * BY_POOL + TPB)
            s0, s1 = part[:, 0, BY_POOL, 0, :, :], part[:, 0, BY_POOL, 1, :, :]
            gb = gbB[:, BY_POOL:BY_POOL + 1, :].broadcast_to([P, TPB, H])
            pool.wait_ge(v_pair, 1)
            pool.wait_ge(sum_ld[0][BY_POOL], 32)
            clear()
            link(nc.gpsimd.tensor_tensor(s0, s0, s1, ALU.add))
            link(nc.gpsimd.tensor_tensor(s0, s0, gb, ALU.mult))
            nc.gpsimd.tensor_tensor(x_sb[:, ts, :], x_sb[:, ts, :], s0, ALU.add).then_inc(g_out, 1)

        @block.scalar
        def _(act):
            link, clear = linker(act, ach)
            act.wait_ge(s_ct, 16)
            nc.scalar.activation(condT[:, 1, :, :], condT[:, 0, :, :], ACT.Tanh, scale=0.5).then_inc(a_tanh, 1)
            nc.scalar.preload_act_table_set("natural_log_exp_and_others")

            def rstd_guess(rs):
                link(nc.scalar.activation(rs[:, 1, :], rs[:, 0, :], ACT.Ln))
                return nc.scalar.activation(rs[:, 2, :], rs[:, 1, :], ACT.Exp, scale=-0.5)

            act.wait_ge(v_var1, 1)
            rstd_guess(rs1[:, :, 0:TPB]).then_inc(a_rs1, 1)
            act.wait_ge(v_modT, 1)

            def front(it):
                act.wait_ge(p_xnT, it + 1)
                for k in range(HC):
                    nc.scalar.activation(h1T[:, k, :], bank[3][:, k * S:(k + 1) * S], ACT.Identity,
                                         bias=modT[:, k, bass.ts(it, 1)], scale=modT[:, 2 + k, bass.ts(it, 1)]).then_inc(a_h1T, 1)

            def high(it, t):
                act.wait_ge(v_rope, TPB * it + t + 1)
                nc.scalar.activation(q_split[:, t, :, 0:2, :], rope_part(t, 0), ACT.Copy).then_inc(a_hi, 1)
                nc.scalar.activation(k_split[:, t, :, 0::2, :], rope_part(t, 1), ACT.Copy).then_inc(a_hi, 1)

            def softmax(b, it):
                n = 0
                for g in range(4):
                    if g >= 2:
                        act.wait_ge(p_pv, 4 * b + g - 1)
                    for part in range(3):
                        act.wait_ge(p_s2, 12 * b + n + 1)
                        dst = probT[:, g % 2, part * 512:(part + 1) * 512]
                        nc.scalar.activation(dst, bank[4 + n % 3][:, :], ACT.Exp, scale=SCALE).then_inc(a_exp, 1)
                        n += 1
                    if it is not None and g in (1, 2):
                        high(it, g - 1)
                    if g >= 2:
                        half = g - 2
                        act.wait_ge(p_pv, 4 * b + 2 * half + 2)
                        nc.scalar.activation(att_sb[:, half, :], bank[7][:, :], ACT.Copy).then_inc(a_att, 1)

            def v_copy(it):
                act.wait_ge(p_qkv, TPB * (it + 1))
                nc.scalar.activation(v_aug[:, :, :, 0:D], bank[3][:, :].rearrange("p (t h d) -> p t h d", t=TPB, h=NH),
                                     ACT.Copy).then_inc(a_vaug, 1)

            def k_copy(it, t):
                act.wait_ge(p_qkT, 4 * it + 2 * t + 2)
                src = bank16[(0, 3)[t]].rearrange("p (g q) -> p g q", q=P)
                nc.scalar.activation(kT[:, :, t * P:(t + 1) * P], src, ACT.Copy).then_inc(a_kT, 1)

            def att_copy(ts, n, alt):
                act.wait_ge(p_attT, n)
                q = slice(ts[0] * P, (ts[-1] + 1) * P)
                nc.scalar.activation(attT[:, :, q], back_bank("attT", alt)[:, :].rearrange("p (k q) -> p k q", k=HC)[:, :, q],
                                     ACT.Copy).then_inc(a_attT, 1)

            def rstd(ts, n):
                act.wait_ge(v_x2, n)
                rstd_guess(rs2[:, :, tiles(ts)]).then_inc(a_rs2, 1)

            def h2_copy(ts, n, alt):
                act.wait_ge(p_h2T, n)
                q = slice(ts[0] * P, (ts[-1] + 1) * P)
                nc.scalar.activation(h2T[:, :, q], back_bank("h2T", alt)[:, :].rearrange("p (k q) -> p k q", k=HC)[:, :, q],
                                     ACT.Copy).then_inc(a_h2T, 1)

            def exp_sums(ts, n):
                act.wait_ge(v_top, n)
                for t in ts:
                    nc.scalar.activation(exp8[:, t, :], top8[:, t, :], ACT.Exp, bias=rows[:, t, H:H + 1],
                                         accum_out=sum8[:, t:t + 1]).then_inc(a_sum, 1)

            def negs(it):
                act.wait_ge(p_negT, it + 1)
                nc.scalar.activation(negT, bankb[0][:, 0:S], ACT.Copy).then_inc(a_negT, 1)

            front(0)
            act.wait_ge(v_var1, 2)
            rstd_guess(rs1[:, :, TPB:2 * TPB]).then_inc(a_rs1, 1)
            high(0, 0)
            high(0, 1)
            act.wait_ge(p_mod, 1)
            for n in range(1, 3):
                nc.scalar.activation(mod_sb[:, n * 512:(n + 1) * 512], bank[5 + n][0:B, :], ACT.Copy).then_inc(a_mod, 1)
            act.wait_ge(g_csts, 1)
            v_copy(0)
            k_copy(0, 0)
            k_copy(0, 1)
            front(1)
            negs(0)
            act.wait_ge(v_var1, 3)
            rstd_guess(rs1[:, :, 2 * TPB:]).then_inc(a_rs1, 1)

            def one_round(it, more):
                softmax(it - 1, it)
                v_copy(it)
                k_copy(it, 0)
                att_copy(ALL, it, 0)
                k_copy(it, 1)
                if more:
                    front(it + 1)
                rstd(ALL, it)
                h2_copy(ALL, it, 0)
                exp_sums(ALL, it)
                negs(it)

            with act.Fori(1, B - 1) as it:
                clear()
                one_round(it, True)
            clear()
            one_round(B - 1, False)
            softmax(B - 1, None)
            for t in ALL:
                att_copy((t,), B + t, t)
            rstd((0,), B)
            h2_copy((0,), B, 0)
            rstd((1,), B + 1)
            exp_sums((0,), B)
            h2_copy((1,), B + 1, 1)
            exp_sums((1,), B + 1)
            nc.scalar.preload_act_table_set("exp_and_others")

            def expert_steps(i, j, first, last):
                s = GRP * i + j
                if not last:
                    act.wait_ge(p_xeT, s + 1)
                    if not (first and j < 2):
                        act.wait_ge(p_gu, s - 1)
                    nc.scalar.activation(xeT[:, j % 2, :], bank[j % 2][:, 0:HC * CAP], ACT.Copy).then_inc(a_xeT, 1)
                if not (first and j < 1) and not (last and j > 0):
                    q = (j - 1) % GRP
                    act.wait_ge(p_gu, s)
                    act.wait_ge(v_meta, s)
                    if not (first and j < 3):
                        act.wait_ge(v_hid, s - 2)
                    nc.scalar.activation(tanhg[:, q % 2, :], bank[2 + q % 2][:, 0:I], ACT.Tanh, scale=0.5).then_inc(a_tg, 1)
                    if not first:
                        act.wait_ge(v_ye, s - GRP + (j == 0))
                    nc.scalar.activation(gatew[:, q:q + 1], bank[2 + q % 2][:, GU:GU + 1], ACT.Exp,
                                         bias=meta[:, q, 0:1]).then_inc(a_w, 1)
                if not (first and j < 2) and not (last and j > 1):
                    q = (j - 2) % GRP
                    act.wait_ge(p_hidT, s - 1)
                    if not (first and j < 4):
                        act.wait_ge(p_ye, s - 3)
                    nc.scalar.activation(hidT[:, q % 2, :], bank[4 + q % 2][0:I, 0:CAP], ACT.Copy).then_inc(a_hidT, 1)

            for j in range(GRP):
                expert_steps(0, j, True, False)
            with act.Fori(1, E // GRP) as i:
                for j in range(GRP):
                    expert_steps(i, j, False, False)
            for j in range(3):
                expert_steps(E // GRP, j, False, True)

        @block.tensor
        def _(pe):
            mm = nc.tensor.matmul
            def keep_warm(n, idle=bank[0]):
                for _ in range(n):
                    mm(idle[:, :], onesb, onesb[:, None, :].broadcast_to([P, 4, P]), start=True, stop=True)

            pe.wait_ge(v_ones, 1)
            keep_warm(13)
            pe.wait_ge(v_silu, 1)
            pe.wait_ge(s_m0, 16)
            for n in range(4):
                for k in range(HC):
                    last = mm(bank[4][:, n * B:(n + 1) * B], wmod_sb[:, k, n * P:(n + 1) * P], condT[:, 3, k, :],
                              start=k == 0, stop=k == HC - 1)
            last.then_inc(p_modT, 1)
            keep_warm(6)
            pe.wait_ge(s_c, 48)

            def mod_rows():
                pe.wait_ge(s_m, 16)
                for n in range(1, 3):
                    for k in range(HC):
                        last = mm(bank[5 + n][0:B, :], condT[:, 3, k, :], wmod_sb[:, k, n * 512:(n + 1) * 512],
                                  start=k == 0, stop=k == HC - 1)
                last.then_inc(p_mod, 1)

            def front(it):
                if not isinstance(it, int) or it > 0:
                    pe.wait_ge(a_kT, TPB * it)
                pe.wait_ge(v_xn, it + 1)
                for t in range(TPB):
                    for k in range(HC):
                        last = nc.tensor.transpose(bank[3][:, k * S + t * P:k * S + (t + 1) * P],
                                                   xn[:, t, k * P:(k + 1) * P], ident)
                last.then_inc(p_xnT, 1)

            def qkv(it, t, what=(0, 1)):
                pe.wait_ge(a_h1T, HC * (it + 1))
                for n in what:
                    dst, c0, c1 = ((bank[1 + t][:, :], 0, 2 * H), (bank[3][:, t * H:(t + 1) * H], 2 * H, 3 * H))[n]
                    for k in range(HC):
                        mm(dst, h1T[:, k, t * P:(t + 1) * P], wqkv_sb[:, k, c0:c1], start=k == 0, stop=False)
                    last = mm(dst, ones3, bias3[:, c0:c1], start=False, stop=True)
                if 1 in what:
                    last.then_inc(p_qkv, 1)

            def split_transposes(it, t):
                pe.wait_ge(v_split, TPB * it + t + 1)
                if t == 1:
                    pe.wait_ge(a_vaug, it + 1)
                for src, bk in ((q_split, (1, 2)[t]), (k_split, (0, 3)[t])):
                    flat = src[:, t, :, :, :].rearrange("p h a c -> p (h a c)")
                    for g in range(NH // 2):
                        last = nc.tensor.transpose(bank16[bk][:, g * P:(g + 1) * P], flat[:, g * P:(g + 1) * P], ident16)
                    last.then_inc(p_qkT, 1)

            def scores_for_max(it, n0, n1, b):
                for n in range(n0, n1):
                    g, i0, nh, qt = chunks[n]
                    if n in (0, 4):
                        pe.wait_ge(v_qT, TPB * it + qt + 1)
                        pe.wait_ge(a_kT, TPB * it + qt + 1)
                    r = slice(row0[g], row0[g] + 64)
                    heads = groups[g][i0:i0 + nh]
                    bk = bank[4 + n % 3]
                    if n >= 3:
                        pe.wait_ge(v_max, 12 * it + n - 2)
                    elif b is None and n == 2:
                        pe.wait_ge(a_mod, 2)
                    w = (qt + 1) * P
                    view = bk[:, 0:len(heads) * w].rearrange("p (h k) -> p h k", k=w)
                    mm(view[:, :, w - P:w], identb, maskb[:, None, :].broadcast_to([P, len(heads), P]),
                       start=True, stop=False, skip_group_check=True)
                    for i, h in enumerate(heads):
                        last = mm(view[:, i, :], qT[r, h // 2, qt * P:(qt + 1) * P], kT[r, h // 2, 0:w],
                                  start=False, stop=i == len(heads) - 1, skip_group_check=True)
                    last.then_inc(p_s1, 1)

            def neg_transposes(it):
                pe.wait_ge(v_neg, it + 1)
                for t in range(TPB):
                    last = nc.tensor.transpose(bankb[0][:, t * P:(t + 1) * P],
                                               neg2[:, t, :, :, :].rearrange("p a c h -> p (a c h)"), identb)
                last.then_inc(p_negT, 1)

            def attend(b):
                pe.wait_ge(a_negT, b + 1)
                n = 0

                def pv(g):
                    if g == 0:
                        pe.wait_ge(v_rank, b + 1)
                    pe.wait_ge(a_exp, 12 * b + 3 * g + 3)
                    if g == 2:
                        pe.wait_ge(a_att, 2 * b + 1)
                    for kt in range(TPB):
                        for i, h in enumerate(groups[g]):
                            c = (g % 2) * S
                            src = (probT[:, g % 2, i * S:(i + 1) * S] if kt == 0 else
                                   probT[:, g % 2, 4 * S + i * P:4 * S + (i + 1) * P])
                            last = mm(bank[7][32 * i:32 * i + 32, c + kt * P:c + S], v_aug[:, kt, h, :], src,
                                      start=kt == 0, stop=kt == TPB - 1, skip_group_check=True)
                    last.then_inc(p_pv, 1)

                for g in range(4):
                    r = slice(row0[g], row0[g] + 64)
                    rn = slice(row0[g], row0[g] + 32)
                    for heads, kt in ((groups[g][0:2], 0), (groups[g][2:4], 0), (groups[g], 1)):
                        bk = bank[4 + n % 3]
                        if n >= 3:
                            pe.wait_ge(a_exp, 12 * b + n - 2)
                        w = (TPB - kt) * P
                        view = bk[:, 0:len(heads) * w].rearrange("p (h q) -> p h q", q=w)
                        mm(view[:, :, 0:P], identb, maskTb[:, None, :].broadcast_to([P, len(heads), P]),
                           start=True, stop=False, skip_group_check=True)
                        for i, h in enumerate(heads):
                            mm(view[:, i, :], kT[r, h // 2, kt * P:(kt + 1) * P], qT[r, h // 2, kt * P:S],
                               start=False, stop=False, skip_group_check=True)
                            last = mm(view[:, i, :], pickb[rn, h, :], negT[rn, kt * P:S],
                                      start=False, stop=i == len(heads) - 1, skip_group_check=True)
                        last.then_inc(p_s2, 1)
                        n += 1
                    if g > 0:
                        pv(g - 1)
                pv(3)

            def att_transposes(b):
                pe.wait_ge(a_att, 2 * b + 2)
                for t in range(TPB):
                    for g in range(4):
                        last = nc.tensor.transpose(bank[4 + t][:, g * P:(g + 1) * P],
                                                   att_sb[:, g // 2, (g % 2) * S + t * P:(g % 2) * S + (t + 1) * P], ident)
                    last.then_inc(p_attq, 1)

            def out_transposes(b, ts, alt):
                for t in ts:
                    pe.wait_ge(v_att, TPB * b + t + 1)
                    for k in range(HC):
                        last = nc.tensor.transpose(back_bank("attT", alt)[:, k * S + t * P:k * S + (t + 1) * P],
                                                   att_tok[:, t, k * P:(k + 1) * P], ident)
                last.then_inc(p_attT, 1)

            def o_proj(ts, n, alt):
                pe.wait_ge(a_attT, n)
                for t in ts:
                    dst = back_bank("o", alt)[:, t * H:(t + 1) * H]
                    for k in range(HC):
                        mm(dst, attT[:, k, t * P:(t + 1) * P], wo_sb[:, k, :], start=k == 0, stop=False)
                    last = mm(dst, ones3, bias3[:, 3 * H:4 * H], start=False, stop=True)
                last.then_inc(p_o, 1)

            def h2_transposes(ts, n, alt):
                pe.wait_ge(v_h2, n)
                for t in ts:
                    for k in range(HC):
                        last = nc.tensor.transpose(back_bank("h2T", alt)[:, k * S + t * P:k * S + (t + 1) * P],
                                                   rows[:, t, k * P:(k + 1) * P], ident)
                last.then_inc(p_h2T, 1)

            def router(ts, n, alt):
                pe.wait_ge(a_h2T, n)
                for t in ts:
                    for k in range(HC):
                        last = mm(back_bank("router", alt)[:, t * E:(t + 1) * E], h2T[:, k, t * P:(t + 1) * P],
                                  router_sb[:, k, :], start=k == 0, stop=k == HC - 1)
                last.then_inc(p_log, 1)

            def ranks(ts, n, alt):
                pe.wait_ge(v_sel, n)
                for t in ts:
                    dst = back_bank("router", alt)[:, 256 + t * E:256 + (t + 1) * E]
                    mm(dst, prefixb, sel[:, t, :], start=True, stop=False)
                    last = mm(dst, onesb, seen[:, t, :], start=False, stop=True)
                last.then_inc(p_cum, 1)

            def one_round(it, more):
                b = it - 1
                attend(b)
                split_transposes(it, 0)
                att_transposes(b)
                split_transposes(it, 1)
                out_transposes(b, ALL, 0)
                scores_for_max(it, 0, 2, b)
                o_proj(ALL, it, 0)
                scores_for_max(it, 2, 5, b)
                if more:
                    front(it + 1)
                    keep_warm(4)
                    qkv(it + 1, 0)
                else:
                    keep_warm(12)
                scores_for_max(it, 5, 7, b)
                keep_warm(2)
                h2_transposes(ALL, it, 0)
                scores_for_max(it, 7, 8, b)
                router(ALL, it, 0)
                scores_for_max(it, 8, 11, b)
                if more:
                    qkv(it + 1, 1, (0,))
                else:
                    keep_warm(6)
                ranks(ALL, it, 0)
                scores_for_max(it, 11, 12, b)
                if more:
                    qkv(it + 1, 1, (1,))
                keep_warm(4 if more else 8)
                neg_transposes(it)
                keep_warm(3, bank[4])

            front(0)
            keep_warm(10)
            pe.wait_ge(s_w, 16)
            pe.wait_ge(s_b3, 48)
            qkv(0, 0)
            qkv(0, 1)
            mod_rows()
            keep_warm(4)
            pe.wait_ge(s_w2, 32)
            pe.wait_ge(g_csts, 1)
            split_transposes(0, 0)
            split_transposes(0, 1)
            scores_for_max(0, 0, 3, None)
            front(1)
            scores_for_max(0, 3, 6, None)
            qkv(1, 0)
            scores_for_max(0, 6, 12, None)
            qkv(1, 1)
            pe.wait_ge(g_csts, 2)
            neg_transposes(0)
            with pe.Fori(1, B - 1) as it:
                one_round(it, True)
            one_round(B - 1, False)
            attend(B - 1)
            att_transposes(B - 1)
            for t in ALL:
                out_transposes(B - 1, (t,), t)
                o_proj((t,), B + t, t)
            for t in ALL:
                keep_warm(4)
                h2_transposes((t,), B + t, t)
                router((t,), B + t, t)
                ranks((t,), B + t, t)

            pe.wait_ge(v_slot, TPB * B)
            pe.wait_ge(g_scat, 16 * K * B * TPB)
            keep_warm(7)
            pe.wait_ge(g_rcol, HC)
            pe.wait_ge(s_ew, 16 * 3 * EARLY // GRP)

            def expert_steps(i, j, first, last_):
                s = GRP * i + j
                if not last_:
                    pe.wait_ge(xe_ld[j], 16 * i + 16)
                    if not (first and j < 2):
                        pe.wait_ge(a_xeT, s - 1)
                    for k in range(HC):
                        last = nc.tensor.transpose(bank[j % 2][:, k * CAP:(k + 1) * CAP], xe[:, j, k * P:(k + 1) * P], ident)
                    last.then_inc(p_xeT, 1)
                if not (first and j < 1) and not (last_ and j > 0):
                    q = (j - 1) % GRP
                    pe.wait_ge(a_xeT, s)
                    if not (first and j < 3):
                        pe.wait_ge(v_hid, s - 2)
                        pe.wait_ge(a_w, s - 2)
                    for k in range(HC):
                        last = mm(bank[2 + q % 2][:, 0:GU + 1], xeT[:, q % 2, k * CAP:(k + 1) * CAP],
                                  expert_w[:, s - 1, k * (GU + 1):(k + 1) * (GU + 1)], start=k == 0, stop=k == HC - 1)
                    last.then_inc(p_gu, 1)
                if not (first and j < 2) and not (last_ and j > 1):
                    q = (j - 2) % GRP
                    pe.wait_ge(v_hid, s - 1)
                    if not (first and j < 4):
                        pe.wait_ge(a_hidT, s - 3)
                    nc.tensor.transpose(bank[4 + q % 2][0:I, 0:CAP], hid[:, q % 2, :], ident).then_inc(p_hidT, 1)
                if not (first and j < 3):
                    q = (j - 3) % GRP
                    pe.wait_ge(a_hidT, s - 2)
                    if not (first and j < 5):
                        pe.wait_ge(v_ye, s - 4)
                    mm(bank[6 + q % 2][:, 0:H], hidT[:, q % 2, :], expert_w[0:I, s - 3, HC * (GU + 1):EW],
                       start=True, stop=True).then_inc(p_ye, 1)

            for j in range(GRP):
                expert_steps(0, j, True, False)
            with pe.Fori(1, EARLY // GRP) as i:
                for j in range(GRP):
                    expert_steps(i, j, False, False)
            pe.wait_ge(g_rcol, 2 * HC)
            half = (E - EARLY) // GRP // 2
            pe.wait_ge(s_lw[0], 16 * 3)
            pe.wait_ge(s_lw[1], 16 * 3 * 4)
            with pe.Fori(EARLY // GRP, EARLY // GRP + half) as i:
                for j in range(GRP):
                    expert_steps(i, j, False, False)
            pe.wait_ge(s_lw[2], 16 * 3 * 2 * 4)
            with pe.Fori(EARLY // GRP + half, E // GRP) as i:
                for j in range(GRP):
                    expert_steps(i, j, False, False)
            for j in range(3):
                expert_steps(E // GRP, j, False, True)

        @block.vector
        def _(dve):
            link, clear = linker(dve, vch)
            V = nc.vector
            V.memset(onesb, 1.0).then_inc(v_ones, 1)
            dve.wait_ge(a_tanh, 1)
            link(V.scalar_tensor_tensor(condT[:, 2, :, :], condT[:, 1, :, :], 1.0, condT[:, 0, :, :], ALU.add, ALU.mult))
            V.tensor_scalar(condT[:, 3, :, :], condT[:, 2, :, :], 0.5, None, ALU.mult).then_inc(v_silu, 1)

            def statistics(n0, n1):
                for n in range(n0, n1):
                    link(V.bn_stats(stats[:, n, :], x_sb[:, n, :]))
                for n in range(n0, n1):
                    link(V.bn_aggr(mv1[:, n, :], stats[:, n, :]))
                V.tensor_scalar(rs1[:, 0, n0:n1], mv1[:, n0:n1, 1], EPS, None, ALU.add).then_inc(v_var1, 1)

            def refine(rs):
                link(V.scalar_tensor_tensor(rs[:, 1, :], rs[:, 2, :], -0.5, rs[:, 2, :], ALU.mult, ALU.mult))
                link(V.tensor_tensor(rs[:, 1, :], rs[:, 1, :], rs[:, 0, :], ALU.mult))
                link(V.scalar_tensor_tensor(rs[:, 3, :], rs[:, 1, :], 1.5, rs[:, 2, :], ALU.add, ALU.mult))

            dve.wait_ge(s_x0, 16)
            statistics(0, TPB)
            dve.wait_ge(p_modT, 1)
            modv = bank[4][:, 0:4 * B].rearrange("p (n b) -> p n b", b=B)
            link(V.tensor_copy(modT[:, 0:2, :], modv[:, 0:2, :]))
            V.tensor_scalar(modT[:, 2:4, :], modv[:, 2:4, :], 1.0, None, ALU.add).then_inc(v_modT, 1)
            dve.wait_ge(a_rs1, 1)
            refine(rs1[:, :, 0:TPB])

            def modulation_rows():
                dve.wait_ge(a_mod, 2)
                link(V.tensor_scalar(mod_sb[:, 4 * H:5 * H], mod_sb[:, 4 * H:5 * H], 1.0, None, ALU.add))
                g = mod_sb[:, 2 * H:].rearrange("p (n h) -> p n h", h=H)[:, 0::3, :]
                link(V.tensor_scalar(mod_t[:, 0, :, :], g, 0.0, 2.0, ALU.is_ge, ALU.mult))
                link(V.tensor_scalar(mod_t[:, 0, :, :], mod_t[:, 0, :, :], 1.0, None, ALU.subtract))
                link(V.scalar_tensor_tensor(mod_t[:, 1, :, :], g, -1.0, g, ALU.mult, ALU.max))
                V.scalar_tensor_tensor(g, mod_t[:, 1, :, :], 0.25, mod_t[:, 0, :, :], ALU.max, ALU.mult).then_inc(v_mod, 1)

            def normalise(it):
                for t in range(TPB):
                    n = TPB * it + t
                    ins = V.tensor_scalar(xn[:, t, :], x_sb[:, n, :], mv1[:, n, 0:1], rs1[:, 3, bass.ts(n, 1)],
                                          ALU.subtract, ALU.mult)
                    if t == TPB - 1:
                        ins.then_inc(v_xn, 1)
                    else:
                        link(ins)

            def rope_tile(it, t):
                dve.wait_ge(p_qkv, TPB * it + t + 1)
                qk = bank[1 + t][:, :]
                pairs = qk.rearrange("p (m i two) -> p m i two", i=D // 2, two=2)
                r2 = rope2.rearrange("p (m i two) -> p m i two", i=D // 2, two=2)
                heads = 2 * NH
                cos = rope_sb[:, t, 0, None, :].broadcast_to([P, heads, D])
                sin = rope_sb[:, t, 1, :].rearrange("p (i two) -> p i two", two=2)
                link(V.tensor_tensor(rope1[:, t, :].rearrange("p (m d) -> p m d", d=D),
                                     qk.rearrange("p (m d) -> p m d", d=D), cos, ALU.mult))
                for o in range(2):
                    link(V.tensor_tensor(r2[:, :, :, o], pairs[:, :, :, 1 - o],
                                         sin[:, None, :, o].broadcast_to([P, heads, D // 2]), ALU.mult))
                V.tensor_tensor(rope1[:, t, :], rope1[:, t, :], rope2, ALU.add).then_inc(v_rope, 1)
                dve.wait_ge(v_rope, TPB * it + t + 1)

            def low(it, t):
                dve.wait_ge(a_hi, 2 * (TPB * it + t + 1))
                link(V.tensor_tensor(q_split[:, t, :, 2:4, :], rope_part(t, 0), q_split[:, t, :, 0:2, :], ALU.subtract))
                V.tensor_tensor(k_split[:, t, :, 1::2, :], rope_part(t, 1), k_split[:, t, :, 0::2, :],
                                ALU.subtract).then_inc(v_split, 1)

            def q_copy(it, t):
                dve.wait_ge(p_qkT, 4 * it + 2 * t + 1)
                src = bank16[(1, 2)[t]].rearrange("p (g q) -> p g q", q=P)
                V.tensor_copy(qT[:, :, t * P:(t + 1) * P], src).then_inc(v_qT, 1)

            def maxima(it, n0, n1):
                for n in range(n0, n1):
                    g, i0, nh, qt = chunks[n]
                    par, half = g // 2, g % 2
                    dve.wait_ge(p_s1, 12 * it + n + 1)
                    w = (qt + 1) * P
                    src = bank[4 + n % 3][:, 0:nh * w].rearrange("p (h k) -> p h k", k=w)
                    h0 = par + 8 * half + 2 * i0
                    V.tensor_reduce(rmax[:, qt, h0:h0 + 2 * nh - 1:2], src, AX.X, ALU.max).then_inc(v_max, 1)

            def split_maxima(it):
                dve.wait_ge(v_max, 12 * (it + 1))
                neg = negr[:, :, None, :].broadcast_to([P, TPB, 2, NH])
                link(V.tensor_scalar(negr[:, :, :], rmax[:, :, :], -1.0, None, ALU.mult))
                link(V.tensor_copy(neg2[:, :, :, 0, :], neg))
                V.tensor_tensor(neg2[:, :, :, 1, :], neg, neg2[:, :, :, 0, :], ALU.subtract).then_inc(v_neg, 1)

            def attention_out(b):
                for t in range(TPB):
                    dve.wait_ge(p_attq, TPB * b + t + 1)
                    src = bank[4 + t][:, :].rearrange("p (m c) -> p m c", c=32)
                    link(V.reciprocal(rden[:, t, :], src[:, :, D]))
                    dst = att_tok[:, t, :].rearrange("p (m par d) -> p par m d", par=2, d=D)
                    V.tensor_tensor(dst, src[:, :, 0:D].rearrange("p (par m) d -> p par m d", par=2),
                                    rden[:, t, :].rearrange("p (par m o) -> p par m o", par=2, o=1).broadcast_to([P, 2, NH // 2, D]),
                                    ALU.mult).then_inc(v_att, 1)

            def residual(b, ts, n, alt):
                dve.wait_ge(p_o, n)
                dve.wait_ge(s_mb, 32)
                for_all = tiles(ts)
                xb = x_sb[:, bass.ds(TPB * b + ts[0], len(ts)), :]
                link(V.tensor_tensor(r2[:, for_all, :], back_bank("o", alt)[:, :].rearrange("p (t h) -> p t h", t=TPB)[:, for_all, :],
                                     mrow(b, 0, ts), ALU.mult))
                link(V.tensor_tensor(xb, xb, r2[:, for_all, :], ALU.add))
                for t in ts:
                    link(V.bn_stats(stats[:, t, :], x_sb[:, TPB * b + t, :]))
                for t in ts:
                    link(V.bn_aggr(mv2[:, t, :], stats[:, t, :]))
                V.tensor_scalar(rs2[:, 0, for_all], mv2[:, for_all, 1], EPS, None, ALU.add).then_inc(v_x2, 1)

            def hidden_rows(b, ts, n):
                a = tiles(ts)
                dve.wait_ge(g_free, b + 1)
                dve.wait_ge(a_rs2, n)
                refine(rs2[:, :, a])
                for t in ts:
                    link(V.tensor_scalar(r2[:, t, :], x_sb[:, TPB * b + t, :], mv2[:, t, 0:1], rs2[:, 3, t:t + 1],
                                         ALU.subtract, ALU.mult))
                link(V.tensor_tensor(r2[:, a, :], r2[:, a, :], mrow(b, 2, ts), ALU.mult))
                V.tensor_tensor(rows[:, a, 0:H], r2[:, a, :], mrow(b, 1, ts), ALU.add).then_inc(v_h2, 1)

            def picks(ts, n, alt):
                a = tiles(ts)
                dve.wait_ge(p_log, n)
                link(V.tensor_copy(logit[:, a, :], back_bank("router", alt)[:, 0:TPB * E].rearrange("p (t e) -> p t e", t=TPB)[:, a, :]))
                for t in ts:
                    link(V.max(top8[:, t, :], logit[:, t, :]))
                V.tensor_scalar(rows[:, a, H:H + 1], top8[:, a, 0:1], -1.0, None, ALU.mult).then_inc(v_top, 1)
                for t in ts:
                    link(V.match_replace(logit_rep[:, t, :], top8[:, t, :], logit[:, t, :], FAR))
                last = V.tensor_tensor(sel[:, a, :], logit[:, a, :], logit_rep[:, a, :], ALU.not_equal)
                for t in ts:
                    if t + 1 < TPB:
                        link(last)
                        last = V.tensor_tensor(seen[:, t + 1, :], seen[:, t, :], sel[:, t, :], ALU.add)
                last.then_inc(v_sel, 1)
                dve.wait_ge(v_sel, n)

            def slots(b, ts, n, alt):
                a = tiles(ts)
                dve.wait_ge(p_cum, n)
                rank = back_bank("router", alt)[:, 256:256 + TPB * E].rearrange("p (t e) -> p t e", t=TPB)[:, a, :]
                link(V.scalar_tensor_tensor(code[:, 0, a, :], rank, float(CAP), sel[:, a, :], ALU.is_le, ALU.mult))
                base = cst[:, None, 4 * P + NH:4 * P + NH + E].broadcast_to([P, len(ts), E])
                V.scalar_tensor_tensor(code[:, 1, a, :], rank, -1.0, base, ALU.mult, ALU.add).then_inc(v_rank, 1)
                dve.wait_ge(v_rank, n + 1)
                link(V.tensor_tensor(code[:, 0, a, :], code[:, 0, a, :], code[:, 1, a, :], ALU.mult))
                if len(ts) == TPB:
                    link(V.tensor_tensor(seen[:, 0, :], seen[:, TPB - 1, :], sel[:, TPB - 1, :], ALU.add))
                for t in ts:
                    link(V.max(code8[:, t, :], code[:, 0, t, :]))
                dve.wait_ge(a_sum, TPB * b + ts[-1] + 1)
                link(V.reciprocal(rows[:, a, H + 1], sum8[:, a]))
                for t in ts:
                    V.tensor_scalar(slot_idx[:, t, :], code8[:, t, :], -1.0, float(BIGSLOT), ALU.mult, ALU.add).then_inc(v_slot, 1)

            def n_chain():
                return chain_count[0]

            chain_count = [0]
            plain_link, plain_clear = link, clear

            def link(ins):
                chain_count[0] += 1
                plain_link(ins)

            def clear():
                chain_count[0] = 0
                plain_clear()

            r2 = rope2.rearrange("p (t h) -> p t h", t=TPB)

            def mrow(b, n, ts):
                return modB[:, bass.ts(b, 1), n * H:(n + 1) * H].broadcast_to([P, len(ts), H])

            normalise(0)
            V.memset(seen[:, :, :], 0.0).then_inc(v_rank, 1)
            dve.wait_ge(v_rank, 1)
            link(V.memset(neg2[:, :, :, :, :], 0.0))
            dve.wait_ge(s_c, 48)
            dve.wait_ge(s_x, 16)
            statistics(TPB, 2 * TPB)
            dve.wait_ge(a_rs1, 2)
            refine(rs1[:, :, TPB:2 * TPB])
            rope_tile(0, 0)
            rope_tile(0, 1)
            low(0, 0)
            low(0, 1)
            normalise(1)
            q_copy(0, 0)
            q_copy(0, 1)
            maxima(0, 0, 4)
            modulation_rows()
            maxima(0, 4, 6)
            maxima(0, 6, 12)
            split_maxima(0)
            statistics(2 * TPB, B * TPB)
            dve.wait_ge(a_rs1, 3)
            refine(rs1[:, :, 2 * TPB:])

            def one_round(it, more):
                b = it - 1
                rope_tile(it, 0)
                rope_tile(it, 1)
                low(it, 0)
                low(it, 1)
                if more:
                    normalise(it + 1)
                q_copy(it, 0)
                attention_out(b)
                q_copy(it, 1)
                maxima(it, 0, 2)
                residual(b, ALL, it, 0)
                maxima(it, 2, 4)
                hidden_rows(b, ALL, it)
                maxima(it, 4, 8)
                picks(ALL, it, 0)
                maxima(it, 8, 12)
                split_maxima(it)
                slots(b, ALL, it, 0)

            with dve.Fori(1, B - 1) as it:
                clear()
                one_round(it, True)
            clear()
            one_round(B - 1, False)
            clear()
            attention_out(B - 1)
            residual(B - 1, (0,), B, 0)
            hidden_rows(B - 1, (0,), B)
            residual(B - 1, (1,), B + 1, 1)
            picks((0,), B, 0)
            slots(B - 1, (0,), B, 0)
            hidden_rows(B - 1, (1,), B + 1)
            picks((1,), B + 1, 1)
            slots(B - 1, (1,), B + 1, 1)

            def expert_steps(i, j, first, last_):
                s = GRP * i + j
                if not last_:
                    dve.wait_ge(xe_ld[j], 16 * i + 16)
                    if not first:
                        dve.wait_ge(added[j % NACC], 16 * (2 * i - 1 + j // NACC))
                    V.tensor_copy(meta[:, j, 0:3], xe[:, j, H:H + 3]).then_inc(v_meta, 1)
                if not (first and j < 1) and not (last_ and j > 0):
                    q = (j - 1) % GRP
                    gu = bank[2 + q % 2]
                    dve.wait_ge(a_w, s)
                    if not (first and j < 3):
                        dve.wait_ge(p_hidT, s - 2)
                    link(V.scalar_tensor_tensor(hid0[:, q % 2, :], tanhg[:, q % 2, :], 1.0, gu[:, 0:I], ALU.add, ALU.mult))
                    V.scalar_tensor_tensor(hid[:, q % 2, :], hid0[:, q % 2, :], 0.5, gu[:, I:GU],
                                           ALU.mult, ALU.mult).then_inc(v_hid, 1)
                if not (first and j < 3):
                    q = (j - 3) % GRP
                    dve.wait_ge(p_ye, s - 2)
                    dve.wait_ge(a_w, s - 2)
                    if not (first and j < 3 + NACC):
                        if isinstance(i, int) and GRP * i + j - 3 - NACC >= E - LAST:
                            before = GRP * i + j - 3 - NACC
                            dve.wait_ge(added[sum_of(before)], 16 * adds_before(before + 1, sum_of(before)))
                        else:
                            dve.wait_ge(added[q % NACC], 16 * (2 * i + (-1 if j < 3 else (j - 3) // NACC)))
                    V.tensor_scalar(ye[:, q % NACC, :], bank[6 + q % 2][:, 0:H], gatew[:, q:q + 1], meta[:, q, 1:2],
                                    ALU.mult, ALU.mult).then_inc(v_ye, 1)

            clear()
            for j in range(GRP):
                expert_steps(0, j, True, False)
            with dve.Fori(1, E // GRP - 1) as i:
                clear()
                for j in range(GRP):
                    expert_steps(i, j, False, False)
            clear()

            def gated(b, pair):
                dve.wait_ge(sum_ld[pair][b], 32)
                ts = slice(TPB * b, TPB * b + TPB)
                s0, s1 = part[:, pair, b, 0, :, :], part[:, pair, b, 1, :, :]
                link(V.tensor_tensor(s0, s0, s1, ALU.add))
                link(V.tensor_tensor(s0, s0, gbB[:, b:b + 1, :].broadcast_to([P, TPB, H]), ALU.mult))
                return V.tensor_tensor(x_sb[:, ts, :], x_sb[:, ts, :], s0, ALU.add)

            for j in range(GRP):
                expert_steps(E // GRP - 1, j, False, False)
            for j in range(3):
                expert_steps(E // GRP, j, False, True)
            gated(BY_POOL, 1).then_inc(v_pair, 1)
            for b in range(B):
                if b != BY_POOL:
                    link(gated(b, 1))
            for b in range(B):
                if b != BY_POOL:
                    gated(b, 0).then_inc(v_out, 1)


def kernel(**inputs):
    import numpy as np
    import concourse.bacc as bacc
    from concourse.bass_utils import run_bass_kernel_spmd

    a = {n.removeprefix("L0_"): np.asarray(v) for n, v in inputs.items()}
    f32 = np.float32
    B, S, H = a["attn_x"].shape
    D, P, E, CAP = 16, 128, a["ffn_router_weight"].shape[0], 128
    half = D // 2
    inv = (1.0 / np.float32(10000.0) ** (np.arange(half, dtype=f32) / f32(half))).astype(f32)
    ang = np.arange(S, dtype=f32)[:, None] * inv[None, :]
    cos = np.repeat(np.cos(ang), 2, axis=-1)
    sin = np.repeat(np.sin(ang), 2, axis=-1)
    sin[:, 0::2] *= -1
    rope = np.stack([cos, sin], 1).astype(f32)
    r = np.arange(P)
    consts = np.concatenate([
        np.eye(P),
        np.where(r[None, :] <= r[:, None], 0.0, -1e30),
        np.where(r[None, :] >= r[:, None], 0.0, -1e30),
        r[:, None] <= r[None, :],
        (r[:, None] % 64 % 16 == np.arange(16)[None, :]) & (r[:, None] % 64 < 32),
        np.broadcast_to(2 * E * CAP + 1 - CAP * np.arange(E), (P, E)),
    ], 1).astype(f32)
    token_ids = (r[:, None] + P * np.arange(B * S // P + 1)[None, :]).astype(np.int32)
    arrays = {
        "x": a["attn_x"],
        "wqkvT": np.ascontiguousarray(np.concatenate([a["attn_Wq"], a["attn_Wk"], a["attn_Wv"]], 0).T),
        "bias": np.concatenate([a["attn_bq"], a["attn_bk"], a["attn_bv"], a["attn_bo"]]).reshape(-1, P),
        "woT": np.ascontiguousarray(a["attn_Wo"].T),
        "routerT": np.ascontiguousarray(a["ffn_router_weight"].T),
        "gate_up": a["ffn_gate_up_proj"],
        "down": a["ffn_down_proj"],
        "cond": np.ascontiguousarray(a["c"].T.reshape(H // P, P, B).transpose(1, 0, 2)),
        "wmod": a["wmod"],
        "rope": rope,
        "consts": consts,
        "token_ids": token_ids,
    }
    nc = bacc.Bacc("TRN2", target_bir_lowering=False, num_devices=1)
    args = [nc.dram_tensor(f"in_{n}", v.shape, mybir.dt.from_np(v.dtype), kind="ExternalInput").ap()
            for n, v in arrays.items()]
    args.append(nc.dram_tensor("out_y", (B, S, H), mybir.dt.float32, kind="ExternalOutput").ap())
    adaln_moe_program(nc, *args)
    got = run_bass_kernel_spmd(nc, [{f"in_{n}": v for n, v in arrays.items()}], core_ids=[0])
    return got.results[0]["out_y"]
```
